# Optimizing a Trainium2 kernel written in Bass

```python
import numpy as np
import jax
import jax.numpy as jnp

def _softmax(x, axis=-1):
    return jax.nn.softmax(x, axis=axis)

def _gelu(x):
    return jax.nn.gelu(x, approximate=True)

def _silu(x):
    return jax.nn.silu(x)

def _sigmoid(x):
    return jax.nn.sigmoid(x)

def _layernorm(x, axis=-1, eps=1e-05):
    m = jnp.mean(x, axis=axis, keepdims=True)
    v = jnp.var(x, axis=axis, keepdims=True)
    return (x - m) / jnp.sqrt(v + eps)

def _scatter_add(tgt, idx, src, axis=0):
    return tgt.at[idx].add(src)

def _segment_sum(src, seg, n):
    return jax.ops.segment_sum(src, seg, n)
kernel_name = 'mk_sandwich_d1_jaxref_r8_0c12e7'

def setup_inputs(seed: int=0):
    np.random.seed(seed)
    _w = jnp.asarray

    def _L0_attn_setup():
        import jax, jax.numpy as jnp
        import numpy as np
        B, S, D, H = (2, 256, 128, 16)
        HD = D // H
        LN_EPS = 1e-05
        key = jax.random.key(seed)
        ks = jax.random.split(key, 8)
        inv = 1.0 / np.sqrt(D)
        return {'embedded': jax.random.normal(ks[0], (B, S, D), dtype=jnp.float32), 'Wq': jax.random.normal(ks[1], (D, D), dtype=jnp.float32) * inv, 'bq': jax.random.normal(ks[2], (D,), dtype=jnp.float32) * 0.01, 'Wk': jax.random.normal(ks[3], (D, D), dtype=jnp.float32) * inv, 'bk': jax.random.normal(ks[4], (D,), dtype=jnp.float32) * 0.01, 'Wv': jax.random.normal(ks[5], (D, D), dtype=jnp.float32) * inv, 'bv': jax.random.normal(ks[6], (D,), dtype=jnp.float32) * 0.01, 'gamma': jnp.ones((D,), dtype=jnp.float32), 'beta': jnp.zeros((D,), dtype=jnp.float32)}
    _L0_attn_in = _L0_attn_setup()

    def _L0_ffn_setup():
        import jax, jax.numpy as jnp
        import numpy as np
        EPS = 1e-08

        def _ternary_linear(x, w):
            alpha = jnp.mean(jnp.abs(w))
            w_t = jnp.sign(w) * (jnp.abs(w) > 0.5 * alpha).astype(w.dtype)
            w_q = w + jax.lax.stop_gradient(w_t - w)
            d = x.shape[-1]
            rms = jnp.sqrt(jnp.sum(x * x, axis=-1, keepdims=True)) / jnp.sqrt(jnp.asarray(d, x.dtype))
            x_norm = x / (rms + EPS)
            return jnp.einsum('bsd,fd->bsf', x_norm, w_q)
        key = jax.random.key(seed)
        k1, k2, k3 = jax.random.split(key, 3)
        d_model, d_ff = (128, 512)
        B, S = (4, 512)
        x = jax.random.normal(k1, (B, S, d_model), dtype=jnp.float32)
        w_up = jax.random.normal(k2, (d_ff, d_model), dtype=jnp.float32) * 0.02
        w_down = jax.random.normal(k3, (d_model, d_ff), dtype=jnp.float32) * 0.02
        return {'x': x, 'w_up': w_up, 'w_down': w_down}
    _L0_ffn_in = _L0_ffn_setup()
    _d = {'L0_attn_embedded': _L0_attn_in['embedded'], 'L0_attn_Wq': _L0_attn_in['Wq'], 'L0_attn_bq': _L0_attn_in['bq'], 'L0_attn_Wk': _L0_attn_in['Wk'], 'L0_attn_bk': _L0_attn_in['bk'], 'L0_attn_Wv': _L0_attn_in['Wv'], 'L0_attn_bv': _L0_attn_in['bv'], 'L0_attn_gamma': _L0_attn_in['gamma'], 'L0_attn_beta': _L0_attn_in['beta'], 'L0_ffn_w_up': _L0_ffn_in['w_up'], 'L0_ffn_w_down': _L0_ffn_in['w_down']}
    _x0 = _d['L0_attn_embedded']
    _d['L0_attn_embedded'] = jax.random.normal(jax.random.fold_in(jax.random.key(seed), 1), (16, 512, 128), dtype=_x0.dtype)
    del _x0
    return _d

def reference(L0_attn_embedded, L0_attn_Wq, L0_attn_bq, L0_attn_Wk, L0_attn_bk, L0_attn_Wv, L0_attn_bv, L0_attn_gamma, L0_attn_beta, L0_ffn_w_up, L0_ffn_w_down):

    def _L0_attn_ref(embedded, Wq, bq, Wk, bk, Wv, bv, gamma, beta):
        import jax, jax.numpy as jnp
        import numpy as np
        B, S, D, H = (2, 256, 128, 16)
        HD = D // H
        LN_EPS = 1e-05
        b, s, d = embedded.shape
        q = embedded @ Wq.T + bq
        k = embedded @ Wk.T + bk
        v = embedded @ Wv.T + bv
        q = q.reshape(b, s, H, HD).transpose(0, 2, 1, 3)
        k = k.reshape(b, s, H, HD).transpose(0, 2, 1, 3)
        v = v.reshape(b, s, H, HD).transpose(0, 2, 1, 3)
        qk = jnp.einsum('bhqd,bhkd->bhqk', q, k)
        qk = jnp.where(jnp.isnan(qk), -jnp.inf, qk)
        qk = qk / jnp.float32(np.sqrt(s))
        p = jax.nn.softmax(qk, axis=-1)
        p = jnp.where(jnp.isnan(p), 0.0, p)
        v = jnp.where(jnp.isnan(v), 0.0, v)
        mask = jnp.triu(jnp.ones((s, s), dtype=p.dtype), k=0)
        p = p * mask
        z = jnp.einsum('bhqk,bhkd->bhqd', p, v)
        z = z.reshape(b, s, d)
        x = embedded + z
        mu = jnp.mean(x, axis=-1, keepdims=True)
        var = jnp.mean(jnp.square(x - mu), axis=-1, keepdims=True)
        out = (x - mu) * jax.lax.rsqrt(var + LN_EPS) * gamma + beta
        return out

    def _L0_ffn_ref(x, w_up, w_down):
        import jax, jax.numpy as jnp
        import numpy as np
        EPS = 1e-08

        def _ternary_linear(x, w):
            alpha = jnp.mean(jnp.abs(w))
            w_t = jnp.sign(w) * (jnp.abs(w) > 0.5 * alpha).astype(w.dtype)
            w_q = w + jax.lax.stop_gradient(w_t - w)
            d = x.shape[-1]
            rms = jnp.sqrt(jnp.sum(x * x, axis=-1, keepdims=True)) / jnp.sqrt(jnp.asarray(d, x.dtype))
            x_norm = x / (rms + EPS)
            return jnp.einsum('bsd,fd->bsf', x_norm, w_q)
        h = jax.nn.gelu(_ternary_linear(x, w_up), approximate=False)
        return _ternary_linear(h, w_down)
    x = L0_attn_embedded
    x = x + _layernorm(_L0_attn_ref(_layernorm(x, axis=-1), L0_attn_Wq, L0_attn_bq, L0_attn_Wk, L0_attn_bk, L0_attn_Wv, L0_attn_bv, L0_attn_gamma, L0_attn_beta), axis=-1)
    x = x + _layernorm(_L0_ffn_ref(_layernorm(x, axis=-1), L0_ffn_w_up, L0_ffn_w_down), axis=-1)
    return x

_drawn_inputs = setup_inputs


def setup_inputs(seed=0):
    import zlib

    import numpy as np

    out = dict(_drawn_inputs(seed))
    spreads = {'L0_attn_gamma': (1.0, 0.2), 'L0_attn_beta': (0.0, 0.1)}
    factors = {'L0_attn_Wq': 8.0,
     'L0_attn_bq': 33.687,
     'L0_attn_Wk': 8.0,
     'L0_attn_bk': 64.0,
     'L0_attn_Wv': 3.872,
     'L0_attn_bv': 36.002}
    for name, (base, spread) in spreads.items():
        noise = np.random.default_rng([zlib.crc32(name.encode()), seed]).standard_normal(out[name].shape)
        drawn = base * np.exp(spread * noise) if base else spread * noise
        out[name] = jnp.asarray(drawn.astype(out[name].dtype))
    for name, factor in factors.items():
        out[name] = (out[name] * factor).astype(out[name].dtype)
    return out
```

```python
from contextlib import ExitStack

import numpy as np

import concourse.bass as bass
from concourse import mybir

F32 = mybir.dt.float32
BF16 = mybir.dt.bfloat16
ALU = mybir.AluOpType
ACT = mybir.ActivationFunctionType
AX_X = mybir.AxisListType.X

P = 128
B, S, D = 16, 512, 128
H, HD = 16, 8
FF = 512
T = S // P
FT = FF // P
PAIRS = H // 2
QUADS = H // 4
UNITS = PAIRS * T
STEPS = QUADS * T
LEAD = 24
LAG = 4
RING = 8
Q_PART = (0, 0, 1, 1, 0, 2)
K_PART = (0, 1, 0, 1, 2, 0)
ROWS = len(Q_PART) * HD
ROWS_ALL = 2 * ROWS
ROWS_M = ROWS_ALL + 4
INV_SQRT_S = float(1.0 / np.float32(np.sqrt(S)))
LN_EPS = 1e-5
RMS_EPS = 1e-8
DMA = 16


class Turn:

    def __init__(self, offset, reg=None):
        self.offset, self.reg = offset, reg

    def plus(self, n):
        return Turn(self.offset + n, self.reg)

    @property
    def buf(self):
        return self.offset % 2

    @property
    def index(self):
        return self.offset if self.reg is None else self.reg * 2 + self.offset

    def count(self, per, n):
        c = per * self.offset + n
        return c if self.reg is None else self.reg * (2 * per) + c


def wait(eng, sem, turn, per, n, then=None):
    c = turn.count(per, n)
    if turn.reg is None and c < 1:
        return
    eng.wait_ge(sem, c)
    if then is not None and turn.reg is not None:
        eng.sem_inc(then, 1)


def build(nc, x, wq, bq, wk, bk, wv, bv, gamma, beta, w_up, w_down, out):
    with ExitStack() as ctx:
        def sb(name, shape, dt=F32):
            return ctx.enter_context(nc.sbuf_tensor(name, shape, dt))

        def sem(name):
            return ctx.enter_context(nc.semaphore(name))

        scoresT = [ctx.enter_context(nc.psum_tensor(f"scoresT{n}", [P, 2, S], F32)) for n in range(2)]
        scores = [ctx.enter_context(nc.psum_tensor(f"scores{n}", [P, S], F32)) for n in range(2)]
        sums = ctx.enter_context(nc.psum_tensor("sums", [P, S], F32))
        misc = ctx.enter_context(nc.psum_tensor("misc", [P, S], F32))
        sums_q = sums[:, :].rearrange("p (r a) -> p a r", a=S // 32)
        misc_t = misc[:, :].rearrange("p (t c) -> p t c", t=T)

        xn_dram = nc.dram_tensor("xn_dram", [B, S, D], F32).ap()
        part_dram = nc.dram_tensor("part_dram", [2, H, ROWS, S], BF16).ap()
        shift_dram = nc.dram_tensor("shift_dram", [2, 2, H // 2, S], BF16).ap()

        ident = sb("ident", [P, P])
        ident16 = sb("ident16", [P, P], BF16)
        ones = sb("ones", [P, P])
        exponents = sb("exponents", [P, 3, T])
        w_nat = sb("w_nat", [P, 3, D])
        wT = sb("wT", [P, 3, D])
        bias = sb("bias", [P, 2])
        bv_b = sb("bv_b", [P, D])
        gamma_b = sb("gamma_b", [P, D])
        beta_b = sb("beta_b", [P, D])
        ff_abs = sb("ff_abs", [P, 2, 2])
        upT = sb("upT", [P, FF])
        downT = sb("downT", [P, FT, D])

        x_in = sb("x_in", [P, T, D])
        stat1 = sb("stat1", [P, T, 6])
        mv1 = sb("mv1", [P, T, 2])
        rs1 = sb("rs1", [P, 2, T])
        valid = sb("valid", [P, 2, T])
        valid_v = sb("valid_v", [P, T])
        xn = sb("xn", [P, T, D])
        xs = sb("xs", [P, T, D])
        neg = sb("neg", [P, T, D])
        xnT = sb("xnT", [P, S])
        qk = sb("qk", [P, 2, S])
        parts = sb("parts", [P, 3, 2, S], BF16)
        v_tok = sb("v_tok", [P, T, D])

        q_rows = [sb(f"q_rows{n}", [P, PAIRS, S], BF16) for n in range(2)]
        k_rows = [sb(f"k_rows{n}", [P, H, S], BF16) for n in range(2)]
        v_one = [sb(f"v_one{n}", [P, T, QUADS, 4, 32]) for n in range(2)]
        v_only = [sb(f"v_only{n}", [P, T, QUADS, 4, 32]) for n in range(2)]
        one_only = [sb(f"one_only{n}", [P, T, 2, 32]) for n in range(2)]
        neg_max = sb("neg_max", [P, H, T])
        shift = [sb(f"shift{g}", [P, 2, H // 2, T], BF16) for g in range(2)]
        shiftT = [sb(f"shiftT{g}", [2 * (H // 2) * T, P], BF16) for g in range(2)]
        probs = [sb(f"probs{n}", [P, 2, S]) for n in range(RING)]
        diag = [sb(f"diag{n}", [P, 2, P]) for n in range(RING)]
        sums_sb = [sb(f"sums_sb{g}", [P, S // 32, 32]) for g in range(2)]
        sums_t = [sb(f"sums_t{g}", [P, S // 32, 2, 16]) for g in range(2)]

        x_res = sb("x_res", [P, T, D])
        xn_res = sb("xn_res", [P, T, D])
        inv_den = sb("inv_den", [P, S // 32, 2])
        z = sb("z", [P, T, D])
        x1 = sb("x1", [P, T, D])
        a_out = sb("a_out", [P, T, D])
        b_out = sb("b_out", [P, T, D])
        y = sb("y", [P, T, D])
        xr = sb("xr", [P, T, D])
        stat = {n: sb(f"stat_{n}", [P, T, 6]) for n in "abcd"}
        mv = {n: sb(f"mv_{n}", [P, T, 2]) for n in "abcd"}
        rs = {n: sb(f"rs_{n}", [P, 4, T]) for n in "abc"}
        xrT = sb("xrT", [P, S])
        up_sb = sb("up_sb", [P, FT, S])
        hT = sb("hT", [P, FT, S])
        h2 = up_sb
        ff_nat = hT[:, 0:2, :]
        ff_pos, ff_neg = up_sb[:, 0, :], up_sb[:, 1, :]
        ssqf = sb("ssqf", [P, S])
        ssq = sb("ssq", [P, T])
        rs_d = sb("rs_d", [P, 6, T])
        t_sb = sb("t_sb", [P, T, D])
        o_sb = sb("o_sb", [P, T, D])

        names = """weights_in ff_in consts_set ident_set ident_made w_transposed w_copied abs_done abs_summed
            thr_done pos_done neg_done tern_done diff_done ternary_done ffT_done ffT_copied rows_cleared zeros_set ones_set""".split()
        names += """x_loaded stat1_done mv1_done eps1_done rs1_done xn_done mr_done valid_done xneg_done xs_done
            xn_stored xnT_ready xnT_copied q_ready q_copied k_ready k_copied v_ready v_added v_done
            hi_done mid_left mid_done low_done parts_stored rows_loaded v_placed""".split()
        names += """scoresT_ready exp_done masked summed sums_copied scores_ready max_done
            shift_hi shift_lo shift_ready shift_copied shift_stored shift_loaded""".split()
        names += """res_loaded sumsT_done inv_done z_scaled zneg_done z_done x1_done
            stata mva epsa rsa norma gam_done beta_done statb mvb epsb rsb normb y_done
            statc mvc epsc powc mulc addc invc rsc xr_done xrT_ready xrT_copied up_ready up_copied gelu_done
            h2_done ssqf_ready ssqf_copied ssq_ready ssq_copied msq_done rmsh_done rmsh_eps invh_done sqh_done
            t_ready t_copied statd mvd vard_done epsd powd rsd normd o_done stored""".split()
        sm = {n: sem("s_" + n) for n in names}
        setup = sm["rows_cleared"]

        def to_rows(src, n):
            return src.rearrange("(o n) -> o n", o=1).broadcast_to([P, n])

        block = ctx.enter_context(nc.Block())

        def turns(eng, body):
            for i in range(-2, 3):
                body(Turn(i))
            with eng.Fori(1, (B - 4) // 2) as k:
                for u in (1, 2):
                    body(Turn(u, k))
            for i in range(B - 3, B + 2):
                body(Turn(i))

        def has(turn, what):
            if turn.reg is not None:
                return True
            i = turn.offset
            return {"attend": 0 <= i < B, "ahead": 0 <= i + 1 < B, "prepare": 0 <= i + 2 < B,
                    "post": 0 <= i - 1 < B, "finish": 0 <= i - 2 < B}[what]

        def units_of_max(turn, s):
            u = s + LEAD
            if u < UNITS:
                return (turn, u) if has(turn, "attend") else None
            return (turn.plus(1), u - UNITS) if has(turn, "ahead") else None

        def step_of(turn, s):
            w = (s - LAG) // 2
            if s % 2:
                return None
            if w < 0:
                return (turn.plus(-1), w + STEPS) if has(turn, "post") else None
            return (turn, w) if has(turn, "attend") else None

        @block.sync
        def _(sp):
            for n, w in enumerate((wq, wk, wv)):
                sp.dma_start(w_nat[:, n, :], w).then_inc(sm["weights_in"], DMA)
            for n, v in enumerate((bq, bk)):
                sp.dma_start(bias[:, n:n + 1], v.rearrange("(d o) -> d o", o=1)).then_inc(sm["weights_in"], DMA)
            for dst, v in ((bv_b, bv), (gamma_b, gamma), (beta_b, beta)):
                sp.dma_start(dst[:, :], to_rows(v, D)).then_inc(sm["weights_in"], DMA)
            sp.dma_start(ff_nat[:, 0, :].rearrange("p (t d) -> p t d", t=FT),
                         w_up.rearrange("(t p) d -> p t d", p=P)).then_inc(sm["ff_in"], DMA)
            sp.dma_start(ff_nat[:, 1, :], w_down).then_inc(sm["ff_in"], DMA)

            def shift_out(b, g):
                wait(sp, sm["shift_copied"], b, 2, g + 1, setup)
                wait(sp, sm["shift_loaded"], b, 4 * DMA, 2 * DMA * (g - 1), setup)
                sp.dma_start(shift_dram[g].rearrange("c h (t q) -> (c h t) q", t=T),
                             shiftT[g][:, :]).then_inc(sm["shift_stored"], DMA)
                wait(sp, sm["shift_stored"], b, 2 * DMA, DMA * (g + 1), setup)
                for hp in range(2):
                    r = ROWS_ALL + 2 * hp
                    sp.dma_start(q_rows[b.buf][r:r + 2, 4 * g:4 * g + 4, :],
                                 shift_dram[g].rearrange("c (r hp) q -> hp c r q", hp=2)[hp]
                                 ).then_inc(sm["shift_loaded"], DMA)

            def body(i):
                post, fin, prep = i.plus(-1), i.plus(-2), i.plus(2)
                if has(i, "prepare"):
                    wait(sp, sm["xn_done"], prep, 1, 0, setup)
                    sp.dma_start(x_in[:, :, :], x[prep.index].rearrange("(t p) d -> p t d", p=P)
                                 ).then_inc(sm["x_loaded"], DMA)
                if has(i, "post"):
                    wait(sp, sm["y_done"], post, 1, 0, setup)
                    wait(sp, sm["xn_stored"], post, DMA, DMA, setup)
                    sp.dma_start(x_res[:, :, :], x[post.index].rearrange("(t p) d -> p t d", p=P)
                                 ).then_inc(sm["res_loaded"], DMA)
                    sp.dma_start(xn_res[:, :, :], xn_dram[post.index].rearrange("(t p) d -> p t d", p=P)
                                 ).then_inc(sm["res_loaded"], DMA)
                if has(i, "finish"):
                    wait(sp, sm["o_done"], fin, 1, 1, setup)
                    sp.dma_start(out[fin.index].rearrange("(t p) d -> p t d", p=P),
                                 o_sb[:, :, :]).then_inc(sm["stored"], DMA)
                if has(i, "prepare"):
                    wait(sp, sm["xn_done"], prep, 1, 1, setup)
                    sp.dma_start(xn_dram[prep.index].rearrange("(t p) d -> p t d", p=P),
                                 xn[:, :, :]).then_inc(sm["xn_stored"], DMA)
                if has(i, "attend"):
                    shift_out(i, 1)
                if has(i, "prepare"):
                    wait(sp, sm["rows_loaded"], prep, 4 * DMA, 0, setup)
                    for which, part_of in ((0, Q_PART), (1, K_PART)):
                        wait(sp, sm["low_done"], prep, 2, which + 1, setup)
                        for slot, part in enumerate(part_of):
                            sp.dma_start(part_dram[which, :, HD * slot:HD * slot + HD, :],
                                         parts[:, part, which, :]).then_inc(sm["parts_stored"], DMA)
                if has(i, "ahead"):
                    shift_out(i.plus(1), 0)
                if has(i, "prepare"):
                    wait(sp, sm["parts_stored"], prep, 12 * DMA, 12 * DMA, setup)
                    wait(sp, sm["scoresT_ready"], i, UNITS, UNITS, setup)
                    if prep.reg is None and prep.offset < 2:
                        sp.wait_ge(sm["rows_cleared"], 1)
                    for which, rows in ((0, q_rows), (1, k_rows)):
                        for hp in range(2):
                            dst = rows[prep.buf][ROWS * hp:ROWS * hp + ROWS, :, :]
                            if which:
                                dst = dst.rearrange("k (r hp) q -> k hp r q", hp=2)[:, hp]
                            sp.dma_start(dst,
                                         part_dram[which].rearrange("(r hp) k q -> hp k r q", hp=2)[hp]
                                         ).then_inc(sm["rows_loaded"], DMA)

            turns(sp, body)
            sp.wait_ge(sm["stored"], DMA * B)
            sp.wait_ge(sm["xn_stored"], DMA * B)

        @block.tensor
        def _(pe):
            reads = []

            def take_misc(reader):
                if reads:
                    wait(pe, *reads[-1])
                reads.append(reader)

            pe.wait_ge(sm["weights_in"], 8 * DMA)
            pe.wait_ge(sm["ident_made"], 2)
            for n in range(3):
                last = nc.tensor.transpose(misc[:, n * P:(n + 1) * P], w_nat[:, n, :], ident[:, :])
            last.then_inc(sm["w_transposed"], 1)
            pe.wait_ge(sm["rows_cleared"], 1)
            pe.wait_ge(sm["abs_done"], 1)
            nc.tensor.matmul(sums[:, 0:2], ones[:, :], ff_abs[:, 0, :], start=True, stop=True
                             ).then_inc(sm["abs_summed"], 1)
            pe.wait_ge(sm["ternary_done"], 2)
            for n in range(2):
                for t in range(FT):
                    last = nc.tensor.transpose(scoresT[0][:, n, t * P:(t + 1) * P],
                                               ff_nat[:, n, t * P:(t + 1) * P], ident[:, :])
            last.then_inc(sm["ffT_done"], 1)
            pe.wait_ge(sm["ffT_copied"], 1)
            pe.wait_ge(sm["w_copied"], 1)

            def score_unit(b, s):
                pair, kt = 2 * (s // 8) + s % 2, (s // 2) % T
                if s % 16 == 0:
                    wait(pe, sm["shift_loaded"], b, 4 * DMA, 2 * DMA * (s // 16 + 1))
                wait(pe, sm["exp_done"], b, UNITS, s - 1)
                for hp in range(2):
                    h = 2 * pair + hp
                    last = nc.tensor.matmul(scoresT[s % 2][:, hp, :], k_rows[b.buf][0:ROWS_M, h, kt * P:(kt + 1) * P],
                                            q_rows[b.buf][0:ROWS_M, pair, :], start=True, stop=True)
                last.then_inc(sm["scoresT_ready"], 1)

            def max_unit(b, u):
                pair, qt = u // T, u % T
                if u == 0:
                    wait(pe, sm["rows_loaded"], b, 4 * DMA, 4 * DMA)
                for hp in range(2):
                    h = 2 * pair + hp
                    wait(pe, sm["max_done"], b, 2 * UNITS, 2 * u - 1 + hp)
                    nc.tensor.matmul(scores[hp][:, :], q_rows[b.buf][0:ROWS_ALL, pair, qt * P:(qt + 1) * P],
                                     k_rows[b.buf][0:ROWS_ALL, h, :], start=True, stop=True
                                     ).then_inc(sm["scores_ready"], 1)

            def sum_step(b, w):
                quad, kt = w // T, w % T
                i, g = quad % 2, quad // 2
                if w == 0:
                    wait(pe, sm["v_placed"], b, 1, 1)
                if i == 0 and kt == 0:
                    wait(pe, sm["sums_copied"], b, 2, g)
                wait(pe, sm["masked"], b, UNITS, 2 * w + 2)
                n = (2 * w) % RING
                first, final = i == 0 and kt == 0, i == 1 and kt == T - 1
                for j in range(4):
                    nc.tensor.matmul(sums[32 * j:32 * j + 32, kt * P:], one_only[b.buf][:, kt, i, :],
                                     probs[n + j // 2][:, j % 2, kt * P:], start=first, stop=False)
                if kt:
                    for j in range(4):
                        nc.tensor.matmul(sums[32 * j:32 * j + 32, 0:kt * P], v_one[b.buf][:, kt, quad, j, :],
                                         probs[n + j // 2][:, j % 2, 0:kt * P], start=False, stop=False)
                for j in range(4):
                    last = nc.tensor.matmul(sums[32 * j:32 * j + 32, kt * P:(kt + 1) * P],
                                            v_only[b.buf][:, kt, quad, j, :], diag[n + j // 2][:, j % 2, :],
                                            start=False, stop=final)
                last.then_inc(sm["summed"], 1)

            def transpose4(src, ready):
                for t in range(T):
                    last = nc.tensor.transpose(misc_t[:, t, :], src(t), ident[:, :])
                last.then_inc(sm[ready], 1)

            def shift_transpose(b, g):
                take_misc((sm["shift_copied"], b, 2, g + 1))
                wait(pe, sm["shift_lo"], b, 2, g + 1, setup)
                nc.tensor.transpose(misc[0:64, 0:64].bitcast(BF16), shift[g][:, :, :, :].rearrange(
                    "p c h t -> p (c h t)"), ident16[:, :]).then_inc(sm["shift_ready"], 1)

            def body(i):
                post, prep = i.plus(-1), i.plus(2)
                reads.clear()
                if has(i.plus(-1), "post"):
                    reads.append((sm["t_copied"], i.plus(-2), 1, 1))
                elif has(i.plus(-1), "ahead"):
                    reads.append((sm["shift_copied"], i, 2, 1))
                for s in range(UNITS):
                    if has(i, "attend"):
                        score_unit(i, s)
                    if units_of_max(i, s):
                        max_unit(*units_of_max(i, s))
                    if step_of(i, s):
                        sum_step(*step_of(i, s))
                    if has(i, "post"):
                        if s == 14:
                            take_misc((sm["xrT_copied"], post, 1, 1))
                            wait(pe, sm["xr_done"], post, 1, 1)
                            transpose4(lambda t: xr[:, t, :], "xrT_ready")
                        if 15 <= s < 15 + FT:
                            f = s - 15
                            take_misc((sm["up_copied"], post, FT, f + 1))
                            if f == 0:
                                wait(pe, sm["xrT_copied"], post, 1, 1)
                            nc.tensor.matmul(misc[:, :], upT[:, f * P:(f + 1) * P], xrT[:, :],
                                             start=True, stop=True).then_inc(sm["up_ready"], 1)
                        if s == 25:
                            take_misc((sm["ssqf_copied"], post, 1, 1))
                            wait(pe, sm["h2_done"], post, FT, FT)
                            for f in range(FT):
                                last = nc.tensor.matmul(misc[32 * f:32 * f + 32, :], ones[:, 0:32], h2[:, f, :],
                                                        start=True, stop=True)
                            last.then_inc(sm["ssqf_ready"], 1)
                        if s == 26:
                            take_misc((sm["ssq_copied"], post, 1, 1))
                            wait(pe, sm["ssqf_copied"], post, 1, 1)
                            for t in range(T):
                                last = nc.tensor.matmul(misc[:, t:t + 1], ssqf[:, t * P:(t + 1) * P], ones[:, 0:1],
                                                        start=True, stop=True)
                            last.then_inc(sm["ssq_ready"], 1)
                        if 27 <= s < 27 + T:
                            t = s - 27
                            if t == 0:
                                take_misc((sm["t_copied"], post, 1, 1))
                                wait(pe, sm["gelu_done"], post, 1, 1)
                            for f in range(FT):
                                last = nc.tensor.matmul(misc_t[:, t, :], hT[:, f, t * P:(t + 1) * P],
                                                        downT[:, f, :], start=f == 0, stop=f == FT - 1)
                            if t == T - 1:
                                last.then_inc(sm["t_ready"], 1)
                    if has(i, "prepare"):
                        if s == 6:
                            take_misc((sm["xnT_copied"], prep, 1, 1))
                            wait(pe, sm["xs_done"], prep, 1, 1)
                            transpose4(lambda t: xs[:, t, :], "xnT_ready")
                        if s == 7:
                            take_misc((sm["q_copied"], prep, 1, 1))
                            wait(pe, sm["xnT_copied"], prep, 1, 1)
                            nc.tensor.matmul(misc[:, :], wT[:, 0, :], xnT[:, :], start=True, stop=True
                                             ).then_inc(sm["q_ready"], 1)
                        if s == 8:
                            take_misc((sm["k_copied"], prep, 1, 1))
                            nc.tensor.matmul(misc[:, :], wT[:, 1, :], xnT[:, :], start=True, stop=True
                                             ).then_inc(sm["k_ready"], 1)
                        if s == 10:
                            take_misc((sm["v_added"], prep, 1, 1))
                            for t in range(T):
                                last = nc.tensor.matmul(misc_t[:, t, :], xnT[:, t * P:(t + 1) * P], wT[:, 2, :],
                                                        start=True, stop=True)
                            last.then_inc(sm["v_ready"], 1)
                    if s == 9 and has(i, "attend"):
                        shift_transpose(i, 1)
                    if s == 24 and has(i, "ahead"):
                        shift_transpose(i.plus(1), 0)

            turns(pe, body)

        @block.scalar
        def _(act):
            act.wait_ge(sm["w_transposed"], 1)
            nc.scalar.copy(wT[:, :, :], misc[:, 0:3 * P].rearrange("p (n d) -> p n d", n=3)
                           ).then_inc(sm["w_copied"], 1)
            act.wait_ge(sm["ffT_done"], 1)
            nc.scalar.copy(upT[:, :], scoresT[0][:, 0, :])
            nc.scalar.copy(downT[:, :, :], scoresT[0][:, 1, :].rearrange("p (t d) -> p t d", t=FT)
                           ).then_inc(sm["ffT_copied"], 1)

            def body(i):
                post, prep = i.plus(-1), i.plus(2)
                for s in range(UNITS):
                    if has(i, "attend"):
                        wait(act, sm["scoresT_ready"], i, UNITS, s + 1)
                        wait(act, sm["summed"], i, STEPS, s // 2 - RING // 2 + 1)
                        nc.scalar.activation(probs[s % RING][:, :, :], scoresT[s % 2][:, :, :], ACT.Exp,
                                             scale=INV_SQRT_S).then_inc(sm["exp_done"], 1)
                    if s == 18 and has(i, "attend"):
                        wait(act, sm["summed"], i, STEPS, STEPS // 2)
                        wait(act, sm["sumsT_done"], i, 2, 0)
                        nc.scalar.copy(sums_sb[0][:, :, :], sums_q).then_inc(sm["sums_copied"], 1)
                    if has(i, "post"):
                        if s == 2:
                            wait(act, sm["summed"], post, STEPS, STEPS)
                            wait(act, sm["sumsT_done"], post, 2, 0)
                            nc.scalar.copy(sums_sb[1][:, :, :], sums_q).then_inc(sm["sums_copied"], 1)
                        if s == 14:
                            wait(act, sm["xrT_ready"], post, 1, 1)
                            wait(act, sm["up_ready"], post, FT, 0)
                            nc.scalar.copy(xrT[:, :], misc[:, :]).then_inc(sm["xrT_copied"], 1)
                        if 15 <= s < 15 + FT:
                            f = s - 15
                            wait(act, sm["up_ready"], post, FT, f + 1)
                            wait(act, sm["ssqf_ready"], post, 1, 0)
                            nc.scalar.copy(up_sb[:, f, :], misc[:, :]).then_inc(sm["up_copied"], 1)
                        if s == 18:
                            wait(act, sm["up_copied"], post, FT, FT)
                            wait(act, sm["t_ready"], post, 1, 0)
                            wait(act, sm["h2_done"], post, FT, 0)
                            nc.scalar.activation(hT[:, :, :], up_sb[:, :, :], ACT.Gelu
                                                 ).then_inc(sm["gelu_done"], 1)
                        if s == 25:
                            wait(act, sm["ssqf_ready"], post, 1, 1)
                            wait(act, sm["ssq_ready"], post, 1, 0)
                            nc.scalar.copy(ssqf[:, :], misc[:, :]).then_inc(sm["ssqf_copied"], 1)
                        if s == 30:
                            wait(act, sm["t_ready"], post, 1, 1)
                            wait(act, sm["normd"], post, 1, 0)
                            nc.scalar.copy(t_sb[:, :, :], misc_t).then_inc(sm["t_copied"], 1)
                    if has(i, "prepare"):
                        if s == 6:
                            wait(act, sm["xnT_ready"], prep, 1, 1)
                            wait(act, sm["v_ready"], prep, 1, 0)
                            nc.scalar.copy(xnT[:, :], misc[:, :]).then_inc(sm["xnT_copied"], 1)
                        for at, which, n in ((7, "q", 0), (8, "k", 1)):
                            if s == at:
                                wait(act, sm[which + "_ready"], prep, 1, 1)
                                wait(act, sm["low_done"], prep, 2, n - 1)
                                nc.scalar.activation(qk[:, n, :], misc[:, :], ACT.Identity, bias=bias[:, n:n + 1],
                                                     scale=1.0).then_inc(sm[which + "_copied"], 1)
                    for at, g, b, part in ((9, 1, i, "attend"), (24, 0, i.plus(1), "ahead")):
                        if s == at and has(i, part):
                            wait(act, sm["shift_ready"], b, 2, g + 1)
                            wait(act, sm["shift_stored"], b, 2 * DMA, DMA * (g - 1))
                            nc.scalar.copy(shiftT[g][:, :], misc[0:64, 0:64].bitcast(BF16)
                                           ).then_inc(sm["shift_copied"], 1)

            turns(act, body)

        @block.vector
        def _(dve):
            dve.wait_ge(sm["ff_in"], 2 * DMA)
            for n in range(2):
                last = nc.vector.tensor_reduce(ff_abs[:, 0, n:n + 1], ff_nat[:, n, :], AX_X, ALU.add,
                                               apply_absolute_value=True)
            last.then_inc(sm["abs_done"], 1)
            dve.wait_ge(sm["abs_summed"], 1)
            nc.vector.tensor_scalar(ff_abs[:, 1, :], sums[:, 0:2], 1.0 / (FF * D), 0.5, ALU.mult, ALU.mult
                                    ).then_inc(sm["thr_done"], 1)
            dve.wait_ge(sm["thr_done"], 1)
            nc.vector.tensor_scalar(ff_abs[:, 0, :], ff_abs[:, 1, :], -1.0, None, ALU.mult
                                    ).then_inc(sm["thr_done"], 1)
            dve.wait_ge(sm["thr_done"], 2)
            for n in range(2):
                nc.vector.tensor_scalar(ff_pos, ff_nat[:, n, :], ff_abs[:, 1, n:n + 1], None, ALU.is_gt
                                        ).then_inc(sm["pos_done"], 1)
                nc.vector.tensor_scalar(ff_neg, ff_nat[:, n, :], ff_abs[:, 0, n:n + 1], None, ALU.is_lt
                                        ).then_inc(sm["neg_done"], 1)
                dve.wait_ge(sm["neg_done"], n + 1)
                nc.vector.tensor_tensor(ff_pos, ff_pos, ff_neg, ALU.subtract
                                        ).then_inc(sm["tern_done"], 1)
                dve.wait_ge(sm["tern_done"], n + 1)
                nc.vector.tensor_tensor(ff_neg, ff_pos, ff_nat[:, n, :], ALU.subtract
                                        ).then_inc(sm["diff_done"], 1)
                dve.wait_ge(sm["diff_done"], n + 1)
                nc.vector.tensor_tensor(ff_nat[:, n, :], ff_nat[:, n, :], ff_neg, ALU.add
                                        ).then_inc(sm["ternary_done"], 1)
                dve.wait_ge(sm["ternary_done"], n + 1)

            def statistics(b, src, st, mv_, st_sem, mv_sem):
                for t in range(T):
                    last = nc.vector.bn_stats(st[:, t, :], src[:, t, :])
                last.then_inc(sm[st_sem], 1)
                wait(dve, sm[st_sem], b, 1, 1, setup)
                for t in range(T):
                    last = nc.vector.bn_aggr(mv_[:, t, :], st[:, t, :])
                last.then_inc(sm[mv_sem], 1)

            def normalise(dst, src, mv_, scale, done):
                for t in range(T):
                    last = nc.vector.tensor_scalar(dst[:, t, :], src[:, t, :], mv_[:, t, 0:1], scale[:, t:t + 1],
                                                   ALU.subtract, ALU.mult)
                last.then_inc(sm[done], 1)

            def split_shift(b, g):
                wait(dve, sm["max_done"], b, 2 * UNITS, UNITS * (g + 1))
                wait(dve, sm["shift_ready"], b, 2, g - 1)
                nc.vector.tensor_copy(shift[g][:, 0], neg_max[:, 8 * g:8 * g + 8, :]).then_inc(sm["shift_hi"], 1)
                wait(dve, sm["shift_hi"], b, 2, g + 1)
                nc.vector.tensor_tensor(shift[g][:, 1], neg_max[:, 8 * g:8 * g + 8, :], shift[g][:, 0],
                                        ALU.subtract).then_inc(sm["shift_lo"], 1)
                wait(dve, sm["shift_lo"], b, 2, g + 1)

            def body(i):
                post, fin, prep = i.plus(-1), i.plus(-2), i.plus(2)
                for s in range(UNITS):
                    if units_of_max(i, s):
                        b, u = units_of_max(i, s)
                        for hp in range(2):
                            wait(dve, sm["scores_ready"], b, 2 * UNITS, 2 * u + hp + 1)
                            nc.vector.tensor_reduce(neg_max[:, 2 * (u // T) + hp, u % T:u % T + 1], scores[hp][:, :],
                                                    AX_X, ALU.max, negate=True).then_inc(sm["max_done"], 1)
                        if u % (UNITS // 2) == UNITS // 2 - 1:
                            split_shift(b, u // (UNITS // 2))
                    if has(i, "finish"):
                        if s == 1:
                            wait(dve, sm["rsd"], fin, 1, 1)
                            normalise(t_sb, t_sb, mv["d"], rs_d[:, 5, :], "normd")
                        if s == 2:
                            wait(dve, sm["normd"], fin, 1, 1)
                            wait(dve, sm["stored"], fin, DMA, 0)
                            nc.vector.tensor_tensor(o_sb[:, :, :], t_sb[:, :, :], y[:, :, :], ALU.add
                                                    ).then_inc(sm["o_done"], 1)
                    if has(i, "post"):
                        if s in (0, 4):
                            g = s // 4
                            wait(dve, sm["sums_copied"], post, 2, g + 1)
                            wait(dve, sm["x1_done"], post, 1, 0)
                            nc.vector.transpose(sums_t[g][:, :, :, :].rearrange("p a i c -> p (a i c)"),
                                                sums_sb[g][:, :, :].rearrange("p a r -> p (a r)")
                                                ).then_inc(sm["sumsT_done"], 1)
                            wait(dve, sm["sumsT_done"], post, 2, g + 1)
                            nc.vector.reciprocal(inv_den[:, :, :], sums_t[g][:, :, :, HD]).then_inc(sm["inv_done"], 1)
                            wait(dve, sm["inv_done"], post, 2, g + 1)
                            for i2 in range(2):
                                last = nc.vector.tensor_tensor(
                                    z[:, 2 * g + i2, :].rearrange("p (a c) -> p a c", c=HD), sums_t[g][:, :, i2, 0:HD],
                                    inv_den[:, :, i2].unsqueeze(2).broadcast_to([P, S // 32, HD]), ALU.mult)
                            last.then_inc(sm["z_scaled"], 1)
                        if s == 5:
                            wait(dve, sm["z_scaled"], post, 2, 2)
                            if has(i, "prepare"):
                                wait(dve, sm["xs_done"], prep, 1, 1)
                            nc.vector.tensor_scalar(neg[:, :, :], z[:, :, :], 0.0, None, ALU.min
                                                    ).then_inc(sm["zneg_done"], 1)
                            wait(dve, sm["zneg_done"], post, 1, 1)
                            nc.vector.scalar_tensor_tensor(z[:, :, :], z[:, :, :], 0.0, neg[:, :, :],
                                                           ALU.max, ALU.add).then_inc(sm["z_done"], 1)
                        if s == 7:
                            wait(dve, sm["x1_done"], post, 1, 1)
                            statistics(post, x1, stat["a"], mv["a"], "stata", "mva")
                        if s == 8:
                            wait(dve, sm["rsa"], post, 1, 1)
                            normalise(a_out, x1, mv["a"], rs["a"][:, 1, :], "norma")
                        if s == 11:
                            wait(dve, sm["beta_done"], post, 1, 1)
                            statistics(post, a_out, stat["b"], mv["b"], "statb", "mvb")
                        if s == 12:
                            wait(dve, sm["rsb"], post, 1, 1)
                            normalise(b_out, a_out, mv["b"], rs["b"][:, 1, :], "normb")
                        if s == 13:
                            wait(dve, sm["y_done"], post, 1, 1)
                            statistics(post, y, stat["c"], mv["c"], "statc", "mvc")
                        if s == 14:
                            wait(dve, sm["rsc"], post, 1, 1)
                            normalise(xr, y, mv["c"], rs["c"][:, 3, :], "xr_done")
                        if s == 26:
                            wait(dve, sm["ssq_ready"], post, 1, 1)
                            wait(dve, sm["msq_done"], post, 1, 0)
                            nc.vector.tensor_copy(ssq[:, :], misc[:, 0:T]).then_inc(sm["ssq_copied"], 1)
                        if s == 31:
                            wait(dve, sm["t_copied"], post, 1, 1)
                            wait(dve, sm["vard_done"], post, 1, 0)
                            statistics(post, t_sb, stat["d"], mv["d"], "statd", "mvd")
                    if has(i, "prepare"):
                        if s == 3:
                            wait(dve, sm["x_loaded"], prep, DMA, DMA)
                            statistics(prep, x_in, stat1, mv1, "stat1_done", "mv1_done")
                        if s == 4:
                            wait(dve, sm["rs1_done"], prep, 1, 1)
                            wait(dve, sm["xn_stored"], prep, DMA, 0)
                            normalise(xn, x_in, mv1, rs1[:, 1, :], "xn_done")
                            nc.vector.tensor_tensor(valid[:, 0, :], mv1[:, :, 0], rs1[:, 1, :], ALU.mult
                                                    ).then_inc(sm["mr_done"], 1)
                            wait(dve, sm["mr_done"], prep, 1, 1)
                            nc.vector.tensor_tensor(valid[:, 1, :], valid[:, 0, :], valid[:, 0, :], ALU.is_equal
                                                    ).then_inc(sm["valid_done"], 1)
                            wait(dve, sm["z_done"], post, 1, 0)
                            nc.vector.tensor_scalar(neg[:, :, :], xn[:, :, :], 0.0, None, ALU.min
                                                    ).then_inc(sm["xneg_done"], 1)
                            wait(dve, sm["xneg_done"], prep, 1, 1)
                            wait(dve, sm["xnT_ready"], prep, 1, 0)
                            nc.vector.scalar_tensor_tensor(xs[:, :, :], xn[:, :, :], 0.0, neg[:, :, :],
                                                           ALU.max, ALU.add).then_inc(sm["xs_done"], 1)
                        if s == 10:
                            wait(dve, sm["v_ready"], prep, 1, 1)
                            wait(dve, sm["v_placed"], prep, 1, 0)
                            nc.vector.tensor_tensor(v_tok[:, :, :], misc_t, bv_b[:, :].unsqueeze(1).broadcast_to([P, T, D]),
                                                    ALU.add).then_inc(sm["v_added"], 1)
                            nc.vector.tensor_copy(valid_v[:, :], valid[:, 1, :])
                            wait(dve, sm["v_added"], prep, 1, 1)
                            nc.vector.tensor_tensor(v_tok[:, :, :], v_tok[:, :, :],
                                                    valid[:, 1, :].unsqueeze(2).broadcast_to([P, T, D]), ALU.mult
                                                    ).then_inc(sm["v_done"], 1)

            turns(dve, body)

        @block.gpsimd
        def _(pool):
            nc.gpsimd.memset(ident[:, :], 0.0).then_inc(sm["ident_set"], 1)
            nc.gpsimd.memset(ident16[:, :], 0.0).then_inc(sm["ident_set"], 1)
            for n, e in enumerate((-0.5, 0.5, -1.0)):
                last = nc.gpsimd.memset(exponents[:, n, :], e)
            last.then_inc(sm["consts_set"], 1)
            pool.wait_ge(sm["ident_set"], 2)
            for m in (ident, ident16):
                nc.gpsimd.affine_select(out=m[:, :], in_=m[:, :], compare_op=ALU.not_equal, fill=1.0, base=0,
                                        pattern=[[-1, P]], channel_multiplier=1).then_inc(sm["ident_made"], 1)
            for n in range(2):
                nc.gpsimd.memset(k_rows[n][0:ROWS_ALL, :, :], 0.0)
                nc.gpsimd.memset(v_one[n][:, :, :, :, :], 0.0)
                nc.gpsimd.memset(v_only[n][:, :, :, :, :], 0.0)
                last = nc.gpsimd.memset(one_only[n][:, :, :, :], 0.0)
            last.then_inc(sm["zeros_set"], 1)
            pool.wait_ge(sm["zeros_set"], 1)
            pool.wait_ge(sm["ident_made"], 2)
            for n in range(2):
                nc.gpsimd.memset(k_rows[n][ROWS_ALL:ROWS_M, :, :], 1.0).then_inc(sm["ones_set"], 1)
                pool.wait_ge(sm["ones_set"], 3 * n + 1)
                for hp in range(2):
                    v = k_rows[n][ROWS_ALL:ROWS_M, :, :].rearrange("k (r hp) q -> k hp r q", hp=2)[:, hp]
                    last = nc.gpsimd.affine_select(out=v, in_=v, compare_op=ALU.is_ge, fill=0.0, base=(1, -2)[hp],
                                                   pattern=[[0, PAIRS], [0, S]], channel_multiplier=(-1, 1)[hp]
                                                   ).then_inc(sm["ones_set"], 1)
                    pool.wait_ge(sm["ones_set"], 3 * n + 2 + hp)
            nc.gpsimd.memset(ones[:, :], 1.0).then_inc(sm["rows_cleared"], 1)
            pool.wait_ge(sm["rows_cleared"], 1)

            def rsqrt_of(b, mv_, r, eps_sem, done):
                nc.gpsimd.tensor_scalar(r[:, 0, :], mv_[:, :, 1], LN_EPS, None, ALU.add).then_inc(sm[eps_sem], 1)
                wait(pool, sm[eps_sem], b, 1, 1, setup)
                nc.gpsimd.tensor_tensor(r[:, 1, :], r[:, 0, :], exponents[:, 0, :], ALU.pow).then_inc(sm[done], 1)

            def place_values(b, quad):
                c = 16 * (quad % 2)
                v = v_tok[:, :, 32 * quad:32 * quad + 32].rearrange("p t (j c) -> p t j c", j=4)
                one = valid_v[:, :].unsqueeze(2).unsqueeze(3).broadcast_to([P, T, 4, HD])
                nc.gpsimd.tensor_copy(v_only[b.buf][:, :, quad, :, c:c + HD], v)
                nc.gpsimd.tensor_copy(v_one[b.buf][:, :, quad, :, c:c + HD], v)
                return nc.gpsimd.tensor_copy(v_one[b.buf][:, :, quad, :, c + HD:c + 2 * HD], one)

            def split(b, n, s):
                if s == 0:
                    wait(pool, sm[("q_copied", "k_copied")[n]], b, 1, 1, setup)
                    wait(pool, sm["parts_stored"], b, 12 * DMA, 0, setup)
                    nc.gpsimd.tensor_copy(parts[:, 0, n, :], qk[:, n, :]).then_inc(sm["hi_done"], 1)
                if s == 1:
                    wait(pool, sm["hi_done"], b, 2, n + 1, setup)
                    nc.gpsimd.tensor_tensor(qk[:, n, :], qk[:, n, :], parts[:, 0, n, :], ALU.subtract
                                            ).then_inc(sm["mid_left"], 1)
                if s == 2:
                    wait(pool, sm["mid_left"], b, 2, n + 1, setup)
                    nc.gpsimd.tensor_copy(parts[:, 1, n, :], qk[:, n, :]).then_inc(sm["mid_done"], 1)
                if s == 3:
                    wait(pool, sm["mid_done"], b, 2, n + 1, setup)
                    nc.gpsimd.tensor_tensor(parts[:, 2, n, :], qk[:, n, :], parts[:, 1, n, :], ALU.subtract
                                            ).then_inc(sm["low_done"], 1)

            def body(i):
                post, fin, prep, ahead = i.plus(-1), i.plus(-2), i.plus(2), i.plus(1)
                for s in range(UNITS):
                    if has(i, "attend"):
                        kt = (s // 2) % T
                        wait(pool, sm["exp_done"], i, UNITS, s + 1, setup)
                        wait(pool, sm["summed"], i, STEPS, s // 2 - RING // 2 + 1, setup)
                        nc.gpsimd.affine_select(out=diag[s % RING][:, :, :], in_=probs[s % RING][:, :, kt * P:(kt + 1) * P],
                                                compare_op=ALU.is_ge, fill=0.0, base=0, pattern=[[0, 2], [-1, P]],
                                                channel_multiplier=1).then_inc(sm["masked"], 1)
                    if has(i, "prepare"):
                        if s == 3:
                            wait(pool, sm["mv1_done"], prep, 1, 1, setup)
                            rsqrt_of(prep, mv1, rs1, "eps1_done", "rs1_done")
                        if 13 <= s < 21:
                            split(prep, (s - 13) // 4, (s - 13) % 4)
                    if has(i, "ahead") and 3 <= s < 3 + QUADS:
                        if s == 3:
                            wait(pool, sm["v_done"], ahead, 1, 1, setup)
                            wait(pool, sm["summed"], ahead, STEPS, -STEPS, setup)
                            for i2 in range(2):
                                c = 16 * i2 + HD
                                nc.gpsimd.tensor_copy(one_only[ahead.buf][:, :, i2, c:c + HD],
                                                      valid_v[:, :].unsqueeze(2).broadcast_to([P, T, HD]))
                        last = place_values(ahead, s - 3)
                        if s == 3 + QUADS - 1:
                            last.then_inc(sm["v_placed"], 1)
                    if has(i, "post"):
                        if s == 5:
                            wait(pool, sm["z_done"], post, 1, 1, setup)
                            wait(pool, sm["res_loaded"], post, 2 * DMA, 2 * DMA, setup)
                            wait(pool, sm["norma"], post, 1, 0, setup)
                            nc.gpsimd.tensor_tensor(x1[:, :, :], xn_res[:, :, :], z[:, :, :], ALU.add
                                                    ).then_inc(sm["x1_done"], 1)
                        if s == 7:
                            wait(pool, sm["mva"], post, 1, 1, setup)
                            rsqrt_of(post, mv["a"], rs["a"], "epsa", "rsa")
                        if s == 8:
                            wait(pool, sm["norma"], post, 1, 1, setup)
                            nc.gpsimd.tensor_tensor(a_out[:, :, :], a_out[:, :, :],
                                                    gamma_b[:, :].unsqueeze(1).broadcast_to([P, T, D]), ALU.mult
                                                    ).then_inc(sm["gam_done"], 1)
                        if s == 9:
                            wait(pool, sm["gam_done"], post, 1, 1, setup)
                            nc.gpsimd.tensor_tensor(a_out[:, :, :], a_out[:, :, :],
                                                    beta_b[:, :].unsqueeze(1).broadcast_to([P, T, D]), ALU.add
                                                    ).then_inc(sm["beta_done"], 1)
                        if s == 11:
                            wait(pool, sm["mvb"], post, 1, 1, setup)
                            rsqrt_of(post, mv["b"], rs["b"], "epsb", "rsb")
                        if s == 12:
                            wait(pool, sm["normb"], post, 1, 1, setup)
                            wait(pool, sm["o_done"], post, 1, 0, setup)
                            nc.gpsimd.tensor_tensor(y[:, :, :], x_res[:, :, :], b_out[:, :, :], ALU.add
                                                    ).then_inc(sm["y_done"], 1)
                        if s == 13:
                            r = rs["c"]
                            wait(pool, sm["mvc"], post, 1, 1, setup)
                            nc.gpsimd.tensor_scalar(r[:, 0, :], mv["c"][:, :, 1], LN_EPS, None, ALU.add)
                            nc.gpsimd.tensor_scalar(r[:, 1, :], mv["c"][:, :, 1], 1.0, None, ALU.mult
                                                    ).then_inc(sm["epsc"], 1)
                            wait(pool, sm["epsc"], post, 1, 1, setup)
                            nc.gpsimd.tensor_tensor(r[:, 2:4, :], r[:, 0:2, :], exponents[:, 0:2, :], ALU.pow
                                                    ).then_inc(sm["powc"], 1)
                            wait(pool, sm["powc"], post, 1, 1, setup)
                            nc.gpsimd.tensor_tensor(r[:, 0, :], r[:, 2, :], r[:, 3, :], ALU.mult
                                                    ).then_inc(sm["mulc"], 1)
                            wait(pool, sm["mulc"], post, 1, 1, setup)
                            nc.gpsimd.tensor_scalar(r[:, 1, :], r[:, 0, :], RMS_EPS, None, ALU.add
                                                    ).then_inc(sm["addc"], 1)
                            wait(pool, sm["addc"], post, 1, 1, setup)
                            nc.gpsimd.tensor_tensor(r[:, 0, :], r[:, 1, :], exponents[:, 2, :], ALU.pow
                                                    ).then_inc(sm["invc"], 1)
                            wait(pool, sm["invc"], post, 1, 1, setup)
                            nc.gpsimd.tensor_tensor(r[:, 3, :], r[:, 0, :], r[:, 2, :], ALU.mult
                                                    ).then_inc(sm["rsc"], 1)
                        if 21 <= s < 21 + FT:
                            f = s - 21
                            wait(pool, sm["gelu_done"], post, 1, 1, setup)
                            wait(pool, sm["ssqf_ready"], post, 1, 0, setup)
                            nc.gpsimd.tensor_tensor(h2[:, f, :], hT[:, f, :], hT[:, f, :], ALU.mult
                                                    ).then_inc(sm["h2_done"], 1)
                        if s == 27:
                            wait(pool, sm["ssq_copied"], post, 1, 1, setup)
                            nc.gpsimd.tensor_scalar(rs_d[:, 0, :], ssq[:, :], 1.0 / (32 * FF), None, ALU.mult
                                                    ).then_inc(sm["msq_done"], 1)
                            wait(pool, sm["msq_done"], post, 1, 1, setup)
                            nc.gpsimd.tensor_tensor(rs_d[:, 1, :], rs_d[:, 0, :], exponents[:, 1, :], ALU.pow
                                                    ).then_inc(sm["rmsh_done"], 1)
                            wait(pool, sm["rmsh_done"], post, 1, 1, setup)
                            nc.gpsimd.tensor_scalar(rs_d[:, 0, :], rs_d[:, 1, :], RMS_EPS, None, ALU.add
                                                    ).then_inc(sm["rmsh_eps"], 1)
                            wait(pool, sm["rmsh_eps"], post, 1, 1, setup)
                            nc.gpsimd.tensor_tensor(rs_d[:, 2, :], rs_d[:, 0, :], exponents[:, 2, :], ALU.pow
                                                    ).then_inc(sm["invh_done"], 1)
                            wait(pool, sm["invh_done"], post, 1, 1, setup)
                            nc.gpsimd.tensor_tensor(rs_d[:, 3, :], rs_d[:, 2, :], rs_d[:, 2, :], ALU.mult
                                                    ).then_inc(sm["sqh_done"], 1)
                    if has(i, "finish") and s == 0:
                        wait(pool, sm["mvd"], fin, 1, 1, setup)
                        wait(pool, sm["sqh_done"], fin, 1, 1, setup)
                        nc.gpsimd.tensor_tensor(rs_d[:, 0, :], rs_d[:, 3, :], mv["d"][:, :, 1], ALU.mult
                                                ).then_inc(sm["vard_done"], 1)
                        wait(pool, sm["vard_done"], fin, 1, 1, setup)
                        nc.gpsimd.tensor_scalar(rs_d[:, 1, :], rs_d[:, 0, :], LN_EPS, None, ALU.add
                                                ).then_inc(sm["epsd"], 1)
                        wait(pool, sm["epsd"], fin, 1, 1, setup)
                        nc.gpsimd.tensor_tensor(rs_d[:, 4, :], rs_d[:, 1, :], exponents[:, 0, :], ALU.pow
                                                ).then_inc(sm["powd"], 1)
                        wait(pool, sm["powd"], fin, 1, 1, setup)
                        nc.gpsimd.tensor_tensor(rs_d[:, 5, :], rs_d[:, 4, :], rs_d[:, 2, :], ALU.mult
                                                ).then_inc(sm["rsd"], 1)

            turns(pool, body)


_INS = ["L0_attn_embedded", "L0_attn_Wq", "L0_attn_bq", "L0_attn_Wk", "L0_attn_bk", "L0_attn_Wv", "L0_attn_bv",
        "L0_attn_gamma", "L0_attn_beta", "L0_ffn_w_up", "L0_ffn_w_down"]


def kernel(**inputs):
    import concourse.bacc as bacc
    from concourse.bass_utils import run_bass_kernel_spmd

    nc = bacc.Bacc("TRN2", target_bir_lowering=False, num_devices=1)
    arrays, args = {}, []
    for name in _INS:
        a = np.ascontiguousarray(inputs[name])
        arrays[f"in_{name}_dram"] = a
        args.append(nc.dram_tensor(f"in_{name}_dram", a.shape, mybir.dt.from_np(a.dtype), kind="ExternalInput").ap())
    args.append(nc.dram_tensor("out_0_dram", (B, S, D), F32, kind="ExternalOutput").ap())
    build(nc, *args)
    r = run_bass_kernel_spmd(nc, [arrays], core_ids=[0])
    return r.results[0]["out_0_dram"]
```

```python
from contextlib import ExitStack

import numpy as np

import concourse.bass as bass
from concourse import mybir

F32 = mybir.dt.float32
BF16 = mybir.dt.bfloat16
ALU = mybir.AluOpType
ACT = mybir.ActivationFunctionType
AX_X = mybir.AxisListType.X

P = 128
B, S, D = 16, 512, 128
H, HD = 16, 8
FF = 512
T = S // P
FT = FF // P
PAIRS = H // 2
QUADS = H // 4
UNITS = PAIRS * T
STEPS = QUADS * T
LEAD = 24
LAG = 4
RING = 8
Q_PART = (0, 0, 1, 1, 0, 2)
K_PART = (0, 1, 0, 1, 2, 0)
ROWS = len(Q_PART) * HD
ROWS_ALL = 2 * ROWS
ROWS_M = ROWS_ALL + 4
INV_SQRT_S = float(1.0 / np.float32(np.sqrt(S)))
LN_EPS = 1e-5
XN_BOUND = 12.0
RMS_EPS = 1e-8
DMA = 16


class Turn:

    def __init__(self, offset, reg=None):
        self.offset, self.reg = offset, reg

    def plus(self, n):
        return Turn(self.offset + n, self.reg)

    @property
    def buf(self):
        return self.offset % 2

    @property
    def index(self):
        return self.offset if self.reg is None else self.reg * 2 + self.offset

    def count(self, per, n):
        c = per * self.offset + n
        return c if self.reg is None else self.reg * (2 * per) + c


def wait(eng, sem, turn, per, n, then=None):
    c = turn.count(per, n)
    if turn.reg is None and c < 1:
        return
    eng.wait_ge(sem, c)
    if then is not None and turn.reg is not None:
        eng.sem_inc(then, 1)


def build(nc, x, wq, bq, wk, bk, wv, bv, gamma, beta, w_up, w_down, out):
    with ExitStack() as ctx:
        def sb(name, shape, dt=F32):
            return ctx.enter_context(nc.sbuf_tensor(name, shape, dt))

        def sem(name):
            return ctx.enter_context(nc.semaphore(name))

        scoresT = [ctx.enter_context(nc.psum_tensor(f"scoresT{n}", [P, 2, S], F32)) for n in range(2)]
        scores = [ctx.enter_context(nc.psum_tensor(f"scores{n}", [P, S], F32)) for n in range(2)]
        sums = ctx.enter_context(nc.psum_tensor("sums", [P, S], F32))
        misc = ctx.enter_context(nc.psum_tensor("misc", [P, S], F32))
        sums_q = sums[:, :].rearrange("p (r a) -> p a r", a=S // 32)
        misc_t = misc[:, :].rearrange("p (t c) -> p t c", t=T)

        xn_dram = nc.dram_tensor("xn_dram", [B, S, D], F32).ap()
        part_dram = nc.dram_tensor("part_dram", [2, H, ROWS, S], BF16).ap()
        shift_dram = nc.dram_tensor("shift_dram", [2, 2, H // 2, S], BF16).ap()

        ident = sb("ident", [P, P])
        ident16 = sb("ident16", [P, P], BF16)
        ones = sb("ones", [P, P])
        exponents = sb("exponents", [P, 3, T])
        one_rows = sb("one_rows", [4, 2, S], BF16)
        w_nat = sb("w_nat", [P, 3, D])
        wT = sb("wT", [P, 3, D])
        bias = sb("bias", [P, 2])
        bv_b = sb("bv_b", [P, D])
        bv_v = sb("bv_v", [P, D])
        gamma_b = sb("gamma_b", [P, D])
        beta_b = sb("beta_b", [P, D])
        ff_abs = sb("ff_abs", [P, 2, 2])
        upT = sb("upT", [P, FF])
        downT = sb("downT", [P, FT, D])

        x_in = sb("x_in", [P, T, D])
        stat1 = sb("stat1", [P, T, 6])
        mv1 = sb("mv1", [P, T, 2])
        rs1 = sb("rs1", [P, 4, T])
        valid = sb("valid", [P, T])
        xn = sb("xn", [P, T, D])
        xs = sb("xs", [P, T, D])
        neg = sb("neg", [P, T, D])
        xnT = sb("xnT", [P, S])
        qk = sb("qk", [P, 2, S])
        parts = sb("parts", [P, 3, 2, S], BF16)
        v_tok = sb("v_tok", [P, T, D])

        q_rows = [sb(f"q_rows{n}", [P, PAIRS, S], BF16) for n in range(2)]
        k_rows = [sb(f"k_rows{n}", [P, H, S], BF16) for n in range(2)]
        v_one = [sb(f"v_one{n}", [P, T, 2, 8, 32]) for n in range(2)]
        v_only = [sb(f"v_only{n}", [P, T, 2, 8, 32]) for n in range(2)]
        one_only = [sb(f"one_only{n}", [P, T, 2, 32]) for n in range(2)]
        neg_max = sb("neg_max", [P, H, T])
        shift = [sb(f"shift{g}", [P, 2, H // 2, T], BF16) for g in range(2)]
        shiftT = [sb(f"shiftT{g}", [2 * (H // 2) * T, P], BF16) for g in range(2)]
        probs = [sb(f"probs{n}", [P, 2, S]) for n in range(RING)]
        diag = [sb(f"diag{n}", [P, 2, P]) for n in range(RING)]
        sums_sb = [sb(f"sums_sb{g}", [P, S // 32, 32]) for g in range(2)]
        sums_t = [sb(f"sums_t{g}", [P, S // 32, 2, 16]) for g in range(2)]

        x_res = sb("x_res", [P, T, D])
        xn_res = sb("xn_res", [P, T, D])
        inv_den = sb("inv_den", [P, S // 32, 2])
        z = sb("z", [P, T, D])
        x1 = sb("x1", [P, T, D])
        a_out = sb("a_out", [P, T, D])
        y = [sb(f"y{n}", [P, T, D]) for n in range(2)]
        xr = sb("xr", [P, T, D])
        stat = {n: sb(f"stat_{n}", [P, T, 6]) for n in "abcd"}
        mv = {n: sb(f"mv_{n}", [P, T, 2]) for n in "abcd"}
        rs = {n: sb(f"rs_{n}", [P, 6, T]) for n in "abc"}
        xrT = sb("xrT", [P, S])
        up_sb = sb("up_sb", [P, FT, S])
        hT = sb("hT", [P, FT, S])
        h2 = up_sb
        ff_nat = hT[:, 0:2, :]
        ff_pos, ff_neg = up_sb[:, 0, :], up_sb[:, 1, :]
        ssqf = sb("ssqf", [P, S])
        ssq = sb("ssq", [P, T])
        rs_d = sb("rs_d", [P, 8, T])
        t_sb = sb("t_sb", [P, T, D])
        o_sb = sb("o_sb", [P, T, D])

        names = """weights_in ff_in consts_set ident_set ones_made one_rows_made one_rows_in k_zeroed ident_made w_transposed w_copied abs_done abs_summed
            thr_done pos_done neg_done tern_done diff_done ternary_done ffT_done ffT_copied rows_cleared one_rows_set""".split()
        names += """x_loaded stat1_done mv1_done eps1_done pow1_done rs1_done xn_done valid_done xs_done
            xn_stored xnT_ready xnT_copied q_ready q_copied k_ready k_copied v_ready v_added v_done bv_done
            mid_left mid_done low_done parts_stored rows_loaded v_placed""".split()
        names += """scoresT_ready exp_done masked summed sums_copied scores_ready max_done
            shift_hi shift_lo shift_ready shift_copied shift_stored shift_loaded""".split()
        names += """res_loaded sumsT_done inv_done z_scaled zneg_done z_done x1_done
            stata mva epsa powa rsa norma gam_done beta_done statb mvb epsb powb rsb normb y_done
            statc mvc epsc powc mulc addc invc scalec rsc xr_done xrT_ready xrT_copied up_ready up_copied gelu_done
            h2_done ssqf_ready ssqf_copied ssq_ready ssq_copied msq_done rmsh_done rmsh_eps invh_done sqh_done
            t_ready t_copied statd mvd vard_done epsd powd scaled rsd normd o_done stored""".split()
        sm = {n: sem("s_" + n) for n in names}
        setup = sm["rows_cleared"]

        def to_rows(src, n):
            return src.rearrange("(o n) -> o n", o=1).broadcast_to([P, n])

        block = ctx.enter_context(nc.Block())

        def turns(eng, body):
            for i in range(-2, 3):
                body(Turn(i))
            with eng.Fori(1, (B - 4) // 2) as k:
                for u in (1, 2):
                    body(Turn(u, k))
            for i in range(B - 3, B + 2):
                body(Turn(i))

        def has(turn, what):
            if turn.reg is not None:
                return True
            i = turn.offset
            return {"attend": 0 <= i < B, "ahead": 0 <= i + 1 < B, "prepare": 0 <= i + 2 < B,
                    "post": 0 <= i - 1 < B, "finish": 0 <= i - 2 < B}[what]

        def units_of_max(turn, s):
            u = s + LEAD
            if u < UNITS:
                return (turn, u) if has(turn, "attend") else None
            return (turn.plus(1), u - UNITS) if has(turn, "ahead") else None

        def step_of(turn, s):
            w, half = (s - LAG) // 2, s % 2
            if w < 0:
                return (turn.plus(-1), w + STEPS, half) if has(turn, "post") else None
            return (turn, w, half) if has(turn, "attend") else None

        @block.sync
        def _(sp):
            sp.dma_start(x_in[:, :, :], x[0].rearrange("(t p) d -> p t d", p=P)).then_inc(sm["x_loaded"], DMA)
            for n, w in enumerate((wq, wk, wv)):
                sp.dma_start(w_nat[:, n, :], w).then_inc(sm["weights_in"], DMA)
            for n, v in enumerate((bq, bk)):
                sp.dma_start(bias[:, n:n + 1], v.rearrange("(d o) -> d o", o=1)).then_inc(sm["weights_in"], DMA)
            for dst, v in ((bv_b, bv), (gamma_b, gamma), (beta_b, beta)):
                sp.dma_start(dst[:, :], to_rows(v, D)).then_inc(sm["weights_in"], DMA)
            sp.dma_start(ff_nat[:, 0, :].rearrange("p (t d) -> p t d", t=FT),
                         w_up.rearrange("(t p) d -> p t d", p=P)).then_inc(sm["ff_in"], DMA)
            sp.dma_start(ff_nat[:, 1, :], w_down).then_inc(sm["ff_in"], DMA)
            sp.wait_ge(sm["one_rows_made"], 1)
            for n in range(2):
                for pair in range(PAIRS):
                    sp.dma_start(k_rows[n][ROWS_ALL:ROWS_M, 2 * pair:2 * pair + 2, :], one_rows[:, :, :]
                                 ).then_inc(sm["one_rows_in"], DMA)

            def shift_out(b, g):
                wait(sp, sm["shift_copied"], b, 2, g + 1, setup)
                wait(sp, sm["shift_loaded"], b, 4 * DMA, 2 * DMA * (g - 1), setup)
                sp.dma_start(shift_dram[g].rearrange("c h (t q) -> (c h t) q", t=T),
                             shiftT[g][:, :]).then_inc(sm["shift_stored"], DMA)
                wait(sp, sm["shift_stored"], b, 2 * DMA, DMA * (g + 1), setup)
                for hp in range(2):
                    r = ROWS_ALL + 2 * hp
                    sp.dma_start(q_rows[b.buf][r:r + 2, 4 * g:4 * g + 4, :],
                                 shift_dram[g].rearrange("c (r hp) q -> hp c r q", hp=2)[hp]
                                 ).then_inc(sm["shift_loaded"], DMA)

            def parts_out(b, which, part_of):
                wait(sp, sm["low_done"], b, 2, which + 1, setup)
                for slot, part in enumerate(part_of):
                    sp.dma_start(part_dram[which, :, HD * slot:HD * slot + HD, :],
                                 parts[:, part, which, :]).then_inc(sm["parts_stored"], DMA)

            def body(i):
                post, fin, prep = i.plus(-1), i.plus(-2), i.plus(2)
                if has(i, "post"):
                    wait(sp, sm["y_done"], post, 1, 0, setup)
                    wait(sp, sm["xn_stored"], post, DMA, DMA, setup)
                    sp.dma_start(x_res[:, :, :], x[post.index].rearrange("(t p) d -> p t d", p=P)
                                 ).then_inc(sm["res_loaded"], DMA)
                    sp.dma_start(xn_res[:, :, :], xn_dram[post.index].rearrange("(t p) d -> p t d", p=P)
                                 ).then_inc(sm["res_loaded"], DMA)
                if has(i, "prepare"):
                    wait(sp, sm["xn_done"], prep, 1, 1, setup)
                    sp.dma_start(xn_dram[prep.index].rearrange("(t p) d -> p t d", p=P),
                                 xn[:, :, :]).then_inc(sm["xn_stored"], DMA)
                    if has(i.plus(1), "prepare"):
                        sp.dma_start(x_in[:, :, :], x[prep.plus(1).index].rearrange("(t p) d -> p t d", p=P)
                                     ).then_inc(sm["x_loaded"], DMA)
                if has(i, "attend"):
                    shift_out(i, 1)
                if has(i, "prepare"):
                    wait(sp, sm["rows_loaded"], prep, 4 * DMA, 0, setup)
                    parts_out(prep, 0, Q_PART)
                if has(i, "ahead"):
                    shift_out(i.plus(1), 0)
                if has(i, "prepare"):
                    parts_out(prep, 1, K_PART)
                if has(i, "finish"):
                    wait(sp, sm["o_done"], fin, 1, 1, setup)
                    sp.dma_start(out[fin.index].rearrange("(t p) d -> p t d", p=P),
                                 o_sb[:, :, :]).then_inc(sm["stored"], DMA)
                if has(i, "prepare"):
                    wait(sp, sm["parts_stored"], prep, 12 * DMA, 12 * DMA, setup)
                    wait(sp, sm["scoresT_ready"], i, UNITS, UNITS, setup)
                    if prep.reg is None and prep.offset < 2:
                        sp.wait_ge(sm["k_zeroed"], prep.offset + 1)
                    for which, rows in ((0, q_rows), (1, k_rows)):
                        for hp in range(2):
                            dst = rows[prep.buf][ROWS * hp:ROWS * hp + ROWS, :, :]
                            if which:
                                dst = dst.rearrange("k (r hp) q -> k hp r q", hp=2)[:, hp]
                            sp.dma_start(dst,
                                         part_dram[which].rearrange("(r hp) k q -> hp k r q", hp=2)[hp]
                                         ).then_inc(sm["rows_loaded"], DMA)

            turns(sp, body)
            sp.wait_ge(sm["stored"], DMA * B)
            sp.wait_ge(sm["xn_stored"], DMA * B)

        @block.tensor
        def _(pe):
            reads = []

            def take_misc(reader):
                if reads:
                    wait(pe, *reads[-1])
                reads.append(reader)

            pe.wait_ge(sm["weights_in"], 8 * DMA)
            pe.wait_ge(sm["ident_made"], 2)
            for n in range(3):
                last = nc.tensor.transpose(misc[:, n * P:(n + 1) * P], w_nat[:, n, :], ident[:, :])
            last.then_inc(sm["w_transposed"], 1)
            pe.wait_ge(sm["w_copied"], 1)

            def setup_ff():
                pe.wait_ge(sm["ones_made"], 1)
                pe.wait_ge(sm["abs_done"], 1)
                nc.tensor.matmul(sums[:, 0:2], ones[:, :], ff_abs[:, 0, :], start=True, stop=True
                                 ).then_inc(sm["abs_summed"], 1)
                pe.wait_ge(sm["ternary_done"], 2)
                for n in range(2):
                    for t in range(FT):
                        last = nc.tensor.transpose(scoresT[0][:, n, t * P:(t + 1) * P],
                                                   ff_nat[:, n, t * P:(t + 1) * P], ident[:, :])
                last.then_inc(sm["ffT_done"], 1)

            def score_unit(b, s):
                pair, kt = 2 * (s // 8) + s % 2, (s // 2) % T
                if s == 0 and b.reg is None and b.offset == 0:
                    pe.wait_ge(sm["ffT_copied"], 1)
                    pe.wait_ge(sm["one_rows_in"], DMA * 2 * PAIRS)
                if s % 16 == 0:
                    wait(pe, sm["shift_loaded"], b, 4 * DMA, 2 * DMA * (s // 16 + 1))
                wait(pe, sm["exp_done"], b, UNITS, s - 1)
                for hp in range(2):
                    h = 2 * pair + hp
                    last = nc.tensor.matmul(scoresT[s % 2][:, hp, :], k_rows[b.buf][0:ROWS_M, h, kt * P:(kt + 1) * P],
                                            q_rows[b.buf][0:ROWS_M, pair, :], start=True, stop=True)
                last.then_inc(sm["scoresT_ready"], 1)

            def max_unit(b, u, hp):
                pair, qt = u // T, u % T
                if u == 0 and hp == 0:
                    wait(pe, sm["rows_loaded"], b, 4 * DMA, 4 * DMA)
                wait(pe, sm["max_done"], b, 2 * UNITS, 2 * u - 1 + hp)
                nc.tensor.matmul(scores[hp][:, :], q_rows[b.buf][0:ROWS_ALL, pair, qt * P:(qt + 1) * P],
                                 k_rows[b.buf][0:ROWS_ALL, 2 * pair + hp, :], start=True, stop=True
                                 ).then_inc(sm["scores_ready"], 1)

            def sum_step(b, w, half):
                quad, kt = w // T, w % T
                i, g = quad % 2, quad // 2
                n = (2 * w) % RING
                first, final = i == 0 and kt == 0, i == 1 and kt == T - 1
                if half == 0:
                    if w == 0:
                        wait(pe, sm["v_placed"], b, 1, 1)
                    if first:
                        wait(pe, sm["sums_copied"], b, 2, g)
                    wait(pe, sm["masked"], b, UNITS, 2 * w + 2)
                    for j in range(4):
                        nc.tensor.matmul(sums[32 * j:32 * j + 32, kt * P:], one_only[b.buf][:, kt, i, :],
                                         probs[n + j // 2][:, j % 2, kt * P:], start=first, stop=False)
                    return
                if kt:
                    for j in range(4):
                        nc.tensor.matmul(sums[32 * j:32 * j + 32, 0:kt * P], v_one[b.buf][:, kt, i, 4 * g + j, :],
                                         probs[n + j // 2][:, j % 2, 0:kt * P], start=False, stop=False)
                for j in range(4):
                    last = nc.tensor.matmul(sums[32 * j:32 * j + 32, kt * P:(kt + 1) * P],
                                            v_only[b.buf][:, kt, i, 4 * g + j, :], diag[n + j // 2][:, j % 2, :],
                                            start=False, stop=final)
                last.then_inc(sm["summed"], 1)

            def transpose4(src, ready):
                for t in range(T):
                    last = nc.tensor.transpose(misc_t[:, t, :], src(t), ident[:, :])
                last.then_inc(sm[ready], 1)

            def shift_transpose(b, g):
                take_misc((sm["shift_copied"], b, 2, g + 1))
                wait(pe, sm["shift_lo"], b, 2, g + 1, setup)
                nc.tensor.transpose(misc[0:64, 0:64].bitcast(BF16), shift[g][:, :, :, :].rearrange(
                    "p c h t -> p (c h t)"), ident16[:, :]).then_inc(sm["shift_ready"], 1)

            def body(i):
                post, fin, prep = i.plus(-1), i.plus(-2), i.plus(2)
                reads.clear()
                if has(i.plus(-1), "prepare"):
                    reads.append((sm["v_added"], i.plus(1), 1, 1))
                elif has(i.plus(-1), "post"):
                    reads.append((sm["up_copied"], i.plus(-2), FT, FT))
                elif has(i.plus(-1), "ahead"):
                    reads.append((sm["shift_copied"], i, 2, 1))
                for s in range(UNITS):
                    if units_of_max(i, s):
                        max_unit(*units_of_max(i, s), 0)
                    if step_of(i, s):
                        sum_step(*step_of(i, s))
                    if units_of_max(i, s):
                        max_unit(*units_of_max(i, s), 1)
                    if has(i, "finish"):
                        if 1 <= s < 1 + T:
                            t = s - 1
                            if t == 0:
                                take_misc((sm["t_copied"], fin, 1, 1))
                                wait(pe, sm["gelu_done"], fin, 1, 1)
                            for f in range(FT):
                                last = nc.tensor.matmul(misc_t[:, t, :], hT[:, f, t * P:(t + 1) * P],
                                                        downT[:, f, :], start=f == 0, stop=f == FT - 1)
                            if t == T - 1:
                                last.then_inc(sm["t_ready"], 1)
                        if s == 6:
                            take_misc((sm["ssqf_copied"], fin, 1, 1))
                            wait(pe, sm["h2_done"], fin, FT, FT)
                            for f in range(FT):
                                last = nc.tensor.matmul(misc[32 * f:32 * f + 32, :], ones[:, 0:32], h2[:, f, :],
                                                        start=True, stop=True)
                            last.then_inc(sm["ssqf_ready"], 1)
                        if s == 8:
                            take_misc((sm["ssq_copied"], fin, 1, 1))
                            wait(pe, sm["ssqf_copied"], fin, 1, 1)
                            for t in range(T):
                                last = nc.tensor.matmul(misc[:, t:t + 1], ssqf[:, t * P:(t + 1) * P], ones[:, 0:1],
                                                        start=True, stop=True)
                            last.then_inc(sm["ssq_ready"], 1)
                    if s == 9 and has(i, "attend"):
                        shift_transpose(i, 1)
                    if s == 25 and has(i, "ahead"):
                        shift_transpose(i.plus(1), 0)
                    if has(i, "post"):
                        if s == 26:
                            take_misc((sm["xrT_copied"], post, 1, 1))
                            wait(pe, sm["xr_done"], post, 1, 1)
                            transpose4(lambda t: xr[:, t, :], "xrT_ready")
                        if 27 <= s < 27 + FT:
                            f = s - 27
                            take_misc((sm["up_copied"], post, FT, f + 1))
                            if f == 0:
                                wait(pe, sm["xrT_copied"], post, 1, 1)
                            nc.tensor.matmul(misc[:, :], upT[:, f * P:(f + 1) * P], xrT[:, :],
                                             start=True, stop=True).then_inc(sm["up_ready"], 1)
                    if has(i, "prepare"):
                        if s == 11:
                            take_misc((sm["xnT_copied"], prep, 1, 1))
                            wait(pe, sm["xs_done"], prep, 1, 1)
                            transpose4(lambda t: xs[:, t, :], "xnT_ready")
                        if s == 13:
                            take_misc((sm["q_copied"], prep, 1, 1))
                            wait(pe, sm["xnT_copied"], prep, 1, 1)
                            nc.tensor.matmul(misc[:, :], wT[:, 0, :], xnT[:, :], start=True, stop=True
                                             ).then_inc(sm["q_ready"], 1)
                        if s == 15:
                            take_misc((sm["k_copied"], prep, 1, 1))
                            nc.tensor.matmul(misc[:, :], wT[:, 1, :], xnT[:, :], start=True, stop=True
                                             ).then_inc(sm["k_ready"], 1)
                        if s == 31:
                            take_misc((sm["v_added"], prep, 1, 1))
                            for t in range(T):
                                last = nc.tensor.matmul(misc_t[:, t, :], xnT[:, t * P:(t + 1) * P], wT[:, 2, :],
                                                        start=True, stop=True)
                            last.then_inc(sm["v_ready"], 1)
                            if prep.reg is None and prep.offset == 0:
                                setup_ff()
                    if has(i, "attend"):
                        score_unit(i, s)

            turns(pe, body)

        @block.scalar
        def _(act):
            act.wait_ge(sm["w_transposed"], 1)
            nc.scalar.copy(wT[:, 0:2, :], misc[:, 0:2 * P].rearrange("p (n d) -> p n d", n=2))
            nc.scalar.copy(wT[:, 2, :].rearrange("p (i g c) -> p g i c", i=2, g=2),
                           misc[:, 2 * P:3 * P].rearrange("p (g i c) -> p g i c", i=2, g=2)
                           ).then_inc(sm["w_copied"], 1)
            act.wait_ge(sm["weights_in"], 8 * DMA)
            nc.scalar.copy(bv_v[:, :].rearrange("p (i g c) -> p g i c", i=2, g=2),
                           bv_b[:, :].rearrange("p (g i c) -> p g i c", i=2, g=2)).then_inc(sm["bv_done"], 1)

            def setup_ff():
                act.wait_ge(sm["ffT_done"], 1)
                nc.scalar.copy(upT[:, :], scoresT[0][:, 0, :])
                nc.scalar.copy(downT[:, :, :], scoresT[0][:, 1, :].rearrange("p (t d) -> p t d", t=FT)
                               ).then_inc(sm["ffT_copied"], 1)

            def normalise(dst, src, scale, minus_mean_scale, done):
                for t in range(T):
                    last = nc.scalar.activation(dst[:, t, :], src[:, t, :], ACT.Identity,
                                                bias=minus_mean_scale[:, t:t + 1], scale=scale[:, t:t + 1])
                last.then_inc(sm[done], 1)

            def body(i):
                post, fin, prep, ahead = i.plus(-1), i.plus(-2), i.plus(2), i.plus(1)
                for s in range(UNITS):
                    if s == 19 and has(i, "attend"):
                        wait(act, sm["summed"], i, STEPS, STEPS // 2)
                        wait(act, sm["sumsT_done"], i, 2, 0)
                        nc.scalar.copy(sums_sb[0][:, :, :], sums_q).then_inc(sm["sums_copied"], 1)
                    if has(i, "finish"):
                        if s == 5:
                            wait(act, sm["t_ready"], fin, 1, 1)
                            wait(act, sm["o_done"], fin, 1, 0)
                            nc.scalar.copy(t_sb[:, :, :], misc_t).then_inc(sm["t_copied"], 1)
                        if s == 6:
                            wait(act, sm["ssqf_ready"], fin, 1, 1)
                            wait(act, sm["ssq_ready"], fin, 1, 0)
                            nc.scalar.copy(ssqf[:, :], misc[:, :]).then_inc(sm["ssqf_copied"], 1)
                        if s == 20:
                            wait(act, sm["rsd"], fin, 1, 1)
                            normalise(t_sb, t_sb, rs_d[:, 5, :], rs_d[:, 7, :], "normd")
                    if has(i, "post"):
                        if s == 3:
                            wait(act, sm["summed"], post, STEPS, STEPS)
                            wait(act, sm["sumsT_done"], post, 2, 0)
                            nc.scalar.copy(sums_sb[1][:, :, :], sums_q).then_inc(sm["sums_copied"], 1)
                        if s == 12:
                            wait(act, sm["rsa"], post, 1, 1)
                            wait(act, sm["y_done"], post, 1, 0)
                            normalise(a_out, x1, rs["a"][:, 1, :], rs["a"][:, 3, :], "norma")
                        if s == 18:
                            wait(act, sm["rsb"], post, 1, 1)
                            normalise(a_out, a_out, rs["b"][:, 1, :], rs["b"][:, 3, :], "normb")
                        if s == 24:
                            wait(act, sm["rsc"], post, 1, 1)
                            wait(act, sm["xrT_ready"], post, 1, 0)
                            normalise(xr, y[post.buf], rs["c"][:, 3, :], rs["c"][:, 5, :], "xr_done")
                        if s == 26:
                            wait(act, sm["xrT_ready"], post, 1, 1)
                            wait(act, sm["up_ready"], post, FT, 0)
                            nc.scalar.copy(xrT[:, :], misc[:, :]).then_inc(sm["xrT_copied"], 1)
                        if 27 <= s < 27 + FT:
                            f = s - 27
                            wait(act, sm["up_ready"], post, FT, f + 1)
                            wait(act, sm["ssqf_ready"], post, 1, 0)
                            nc.scalar.copy(up_sb[:, f, :], misc[:, :]).then_inc(sm["up_copied"], 1)
                        if s == 31:
                            wait(act, sm["up_copied"], post, FT, FT)
                            wait(act, sm["t_ready"], post, 1, 0)
                            wait(act, sm["h2_done"], post, FT, 0)
                            nc.scalar.activation(hT[:, :, :], up_sb[:, :, :], ACT.Gelu
                                                 ).then_inc(sm["gelu_done"], 1)
                    if has(i, "ahead") and s == 8:
                        wait(act, sm["v_done"], ahead, 1, 1)
                        for i2 in range(2):
                            c = 16 * i2
                            nc.scalar.copy(v_one[ahead.buf][:, :, i2, :, c:c + HD],
                                           v_only[ahead.buf][:, :, i2, :, c:c + HD])
                            nc.scalar.copy(v_one[ahead.buf][:, :, i2, :, c + HD:c + 2 * HD],
                                           valid[:, :].unsqueeze(2).unsqueeze(3).broadcast_to([P, T, 8, HD]))
                            last = nc.scalar.copy(one_only[ahead.buf][:, :, i2, c + HD:c + 2 * HD],
                                                  valid[:, :].unsqueeze(2).broadcast_to([P, T, HD]))
                        last.then_inc(sm["v_placed"], 1)
                    if has(i, "prepare"):
                        if s == 6:
                            wait(act, sm["rs1_done"], prep, 1, 1)
                            wait(act, sm["xn_stored"], prep, DMA, 0)
                            wait(act, sm["xs_done"], prep, 1, 0)
                            normalise(xn, x_in, rs1[:, 1, :], rs1[:, 3, :], "xn_done")
                        if s == 11:
                            wait(act, sm["xnT_ready"], prep, 1, 1)
                            wait(act, sm["v_ready"], prep, 1, 0)
                            nc.scalar.copy(xnT[:, :], misc[:, :]).then_inc(sm["xnT_copied"], 1)
                        for at, which, n in ((13, "q", 0), (15, "k", 1)):
                            if s == at:
                                wait(act, sm[which + "_ready"], prep, 1, 1)
                                wait(act, sm["low_done"], prep, 2, n - 1)
                                wait(act, sm["parts_stored"], prep, 12 * DMA, 0)
                                nc.scalar.activation(qk[:, n, :], misc[:, :], ACT.Identity, bias=bias[:, n:n + 1],
                                                     scale=1.0)
                                nc.scalar.activation(parts[:, 0, n, :], misc[:, :], ACT.Identity, bias=bias[:, n:n + 1],
                                                     scale=1.0).then_inc(sm[which + "_copied"], 1)
                        if s == 31 and prep.reg is None and prep.offset == 0:
                            setup_ff()
                    for at, g, b, part in ((9, 1, i, "attend"), (25, 0, i.plus(1), "ahead")):
                        if s == at and has(i, part):
                            wait(act, sm["shift_ready"], b, 2, g + 1)
                            wait(act, sm["shift_stored"], b, 2 * DMA, DMA * (g - 1))
                            nc.scalar.copy(shiftT[g][:, :], misc[0:64, 0:64].bitcast(BF16)
                                           ).then_inc(sm["shift_copied"], 1)

                    if has(i, "attend"):
                        wait(act, sm["scoresT_ready"], i, UNITS, s + 1)
                        wait(act, sm["summed"], i, STEPS, s // 2 - RING // 2 + 1)
                        nc.scalar.activation(probs[s % RING][:, :, :], scoresT[s % 2][:, :, :], ACT.Exp,
                                             scale=INV_SQRT_S).then_inc(sm["exp_done"], 1)

            turns(act, body)

        @block.vector
        def _(dve):
            for n in range(2):
                nc.vector.memset(k_rows[n][0:ROWS_ALL, :, :].bitcast(F32), 0.0).then_inc(sm["k_zeroed"], 1)

            def setup_ff():
                dve.wait_ge(sm["ff_in"], 2 * DMA)
                for n in range(2):
                    last = nc.vector.tensor_reduce(ff_abs[:, 0, n:n + 1], ff_nat[:, n, :], AX_X, ALU.add,
                                                   apply_absolute_value=True)
                last.then_inc(sm["abs_done"], 1)
                dve.wait_ge(sm["abs_summed"], 1)
                nc.vector.tensor_scalar(ff_abs[:, 1, :], sums[:, 0:2], 1.0 / (FF * D), 0.5, ALU.mult, ALU.mult
                                        ).then_inc(sm["thr_done"], 1)
                dve.wait_ge(sm["thr_done"], 1)
                nc.vector.tensor_scalar(ff_abs[:, 0, :], ff_abs[:, 1, :], -1.0, None, ALU.mult
                                        ).then_inc(sm["thr_done"], 1)
                dve.wait_ge(sm["thr_done"], 2)
                for n in range(2):
                    nc.vector.tensor_scalar(ff_pos, ff_nat[:, n, :], ff_abs[:, 1, n:n + 1], None, ALU.is_gt
                                            ).then_inc(sm["pos_done"], 1)
                    nc.vector.tensor_scalar(ff_neg, ff_nat[:, n, :], ff_abs[:, 0, n:n + 1], None, ALU.is_lt
                                            ).then_inc(sm["neg_done"], 1)
                    dve.wait_ge(sm["neg_done"], n + 1)
                    nc.vector.tensor_tensor(ff_pos, ff_pos, ff_neg, ALU.subtract
                                            ).then_inc(sm["tern_done"], 1)
                    dve.wait_ge(sm["tern_done"], n + 1)
                    nc.vector.tensor_tensor(ff_neg, ff_pos, ff_nat[:, n, :], ALU.subtract
                                            ).then_inc(sm["diff_done"], 1)
                    dve.wait_ge(sm["diff_done"], n + 1)
                    nc.vector.tensor_tensor(ff_nat[:, n, :], ff_nat[:, n, :], ff_neg, ALU.add
                                            ).then_inc(sm["ternary_done"], 1)
                    dve.wait_ge(sm["ternary_done"], n + 1)

            def statistics(b, src, st, mv_, st_sem, mv_sem, half):
                if half == 0:
                    for t in range(T):
                        last = nc.vector.bn_stats(st[:, t, :], src[:, t, :])
                    last.then_inc(sm[st_sem], 1)
                    return
                wait(dve, sm[st_sem], b, 1, 1, setup)
                for t in range(T):
                    last = nc.vector.bn_aggr(mv_[:, t, :], st[:, t, :])
                last.then_inc(sm[mv_sem], 1)

            def quotient(b, g, half):
                if half == 0:
                    wait(dve, sm["sums_copied"], b, 2, g + 1)
                    nc.vector.transpose(sums_t[g][:, :, :, :].rearrange("p a i c -> p (a i c)"),
                                        sums_sb[g][:, :, :].rearrange("p a r -> p (a r)")
                                        ).then_inc(sm["sumsT_done"], 1)
                    return
                wait(dve, sm["sumsT_done"], b, 2, g + 1)
                nc.vector.reciprocal(inv_den[:, :, :], sums_t[g][:, :, :, HD]).then_inc(sm["inv_done"], 1)
                wait(dve, sm["x1_done"], b, 1, 0)
                wait(dve, sm["inv_done"], b, 2, g + 1)
                for i2 in range(2):
                    last = nc.vector.tensor_tensor(
                        z[:, 2 * g + i2, :].rearrange("p (a c) -> p a c", c=HD), sums_t[g][:, :, i2, 0:HD],
                        inv_den[:, :, i2].unsqueeze(2).broadcast_to([P, S // 32, HD]), ALU.mult)
                last.then_inc(sm["z_scaled"], 1)

            def split_shift(b, g):
                wait(dve, sm["max_done"], b, 2 * UNITS, UNITS * (g + 1))
                wait(dve, sm["shift_ready"], b, 2, g - 1)
                nc.vector.tensor_copy(shift[g][:, 0], neg_max[:, 8 * g:8 * g + 8, :]).then_inc(sm["shift_hi"], 1)
                wait(dve, sm["shift_hi"], b, 2, g + 1)
                nc.vector.tensor_tensor(shift[g][:, 1], neg_max[:, 8 * g:8 * g + 8, :], shift[g][:, 0],
                                        ALU.subtract).then_inc(sm["shift_lo"], 1)
                wait(dve, sm["shift_lo"], b, 2, g + 1)

            def body(i):
                post, fin, prep, ahead = i.plus(-1), i.plus(-2), i.plus(2), i.plus(1)
                for s in range(UNITS):
                    if units_of_max(i, s):
                        b, u = units_of_max(i, s)
                        for hp in range(2):
                            wait(dve, sm["scores_ready"], b, 2 * UNITS, 2 * u + hp + 1)
                            nc.vector.tensor_reduce(neg_max[:, 2 * (u // T) + hp, u % T:u % T + 1], scores[hp][:, :],
                                                    AX_X, ALU.max, negate=True).then_inc(sm["max_done"], 1)
                        if u % (UNITS // 2) == UNITS // 2 - 1:
                            split_shift(b, u // (UNITS // 2))
                    if has(i, "finish"):
                        if s == 8:
                            wait(dve, sm["ssq_ready"], fin, 1, 1)
                            wait(dve, sm["msq_done"], fin, 1, 0)
                            nc.vector.tensor_copy(ssq[:, :], misc[:, 0:T]).then_inc(sm["ssq_copied"], 1)
                        if s == 12:
                            wait(dve, sm["t_copied"], fin, 1, 1)
                        if s in (12, 13):
                            wait(dve, sm["rsd"], fin, 1, 0)
                            statistics(fin, t_sb, stat["d"], mv["d"], "statd", "mvd", s - 12)
                    if has(i, "attend") and s in (23, 24):
                        quotient(i, 0, s - 23)
                    if has(i, "post"):
                        if s in (4, 5):
                            quotient(post, 1, s - 4)
                        if s == 6:
                            wait(dve, sm["z_scaled"], post, 2, 2)
                            nc.vector.tensor_scalar(neg[:, :, :], z[:, :, :], 0.0, None, ALU.min
                                                    ).then_inc(sm["zneg_done"], 1)
                            wait(dve, sm["zneg_done"], post, 1, 1)
                            nc.vector.scalar_tensor_tensor(z[:, :, :], z[:, :, :], 0.0, neg[:, :, :],
                                                           ALU.max, ALU.add).then_inc(sm["z_done"], 1)
                        for at, n, src, ready in ((9, "a", x1, "x1_done"), (15, "b", a_out, "beta_done"),
                                                  (20, "c", y[post.buf], "y_done")):
                            if s == at:
                                wait(dve, sm[ready], post, 1, 1)
                            if s in (at, at + 1):
                                statistics(post, src, stat[n], mv[n], "stat" + n, "mv" + n, s - at)
                    if has(i, "ahead"):
                        if s == 7:
                            wait(dve, sm["v_added"], ahead, 1, 1)
                            wait(dve, sm["valid_done"], ahead, 1, 1)
                            wait(dve, sm["summed"], ahead, STEPS, -STEPS)
                            if ahead.reg is None and ahead.offset == 0:
                                dve.wait_ge(sm["rows_cleared"], 1)
                            for i2 in range(2):
                                c = 16 * i2
                                last = nc.vector.tensor_tensor(
                                    v_only[ahead.buf][:, :, i2, :, c:c + HD],
                                    v_tok[:, :, 64 * i2:64 * i2 + 64].rearrange("p t (h c) -> p t h c", c=HD),
                                    valid[:, :].unsqueeze(2).unsqueeze(3).broadcast_to([P, T, 8, HD]), ALU.mult)
                            last.then_inc(sm["v_done"], 1)
                    if has(i, "prepare"):
                        if s == 1:
                            wait(dve, sm["x_loaded"], prep, DMA, DMA)
                        if s in (1, 2):
                            wait(dve, sm["rs1_done"], prep, 1, 0)
                            statistics(prep, x_in, stat1, mv1, "stat1_done", "mv1_done", s - 1)
                        if s == 8:
                            wait(dve, sm["xn_done"], prep, 1, 1)
                            wait(dve, sm["xnT_ready"], prep, 1, 0)
                            nc.vector.tensor_scalar(xs[:, :, :], xn[:, :, :], -XN_BOUND, XN_BOUND, ALU.max, ALU.min
                                                    ).then_inc(sm["xs_done"], 1)
                        if s == 11:
                            wait(dve, sm["v_placed"], prep, 1, 0)
                            nc.vector.tensor_tensor(valid[:, :], rs1[:, 3, :], rs1[:, 3, :], ALU.is_equal
                                                    ).then_inc(sm["valid_done"], 1)
                        if s == 31:
                            wait(dve, sm["v_ready"], prep, 1, 1)
                            wait(dve, sm["bv_done"], Turn(0), 1, 1)
                            nc.vector.tensor_tensor(v_tok[:, :, :], misc_t, bv_v[:, :].unsqueeze(1).broadcast_to([P, T, D]),
                                                    ALU.add).then_inc(sm["v_added"], 1)
                            if prep.reg is None and prep.offset == 0:
                                setup_ff()

            turns(dve, body)

        @block.gpsimd
        def _(pool):
            nc.gpsimd.memset(ident[:, :], 0.0).then_inc(sm["ident_set"], 1)
            nc.gpsimd.memset(ident16[:, :], 0.0).then_inc(sm["ident_set"], 1)
            for n, e in enumerate((-0.5, 0.5, -1.0)):
                last = nc.gpsimd.memset(exponents[:, n, :], e)
            last.then_inc(sm["consts_set"], 1)
            nc.gpsimd.memset(ones[:, :], 1.0).then_inc(sm["ones_made"], 1)
            nc.gpsimd.memset(one_rows[:, :, :], 1.0).then_inc(sm["one_rows_set"], 1)
            pool.wait_ge(sm["ident_set"], 2)
            for m in (ident, ident16):
                nc.gpsimd.affine_select(out=m[:, :], in_=m[:, :], compare_op=ALU.not_equal, fill=1.0, base=0,
                                        pattern=[[-1, P]], channel_multiplier=1).then_inc(sm["ident_made"], 1)
            pool.wait_ge(sm["one_rows_set"], 1)
            for hp in range(2):
                last = nc.gpsimd.affine_select(out=one_rows[:, hp, :], in_=one_rows[:, hp, :], compare_op=ALU.is_ge,
                                               fill=0.0, base=(1, -2)[hp], pattern=[[0, S]],
                                               channel_multiplier=(-1, 1)[hp])
            last.then_inc(sm["one_rows_made"], 1)
            for n in range(2):
                nc.gpsimd.memset(v_one[n][:, :, :, :, :], 0.0)
                nc.gpsimd.memset(v_only[n][:, :, :, :, :], 0.0)
                last = nc.gpsimd.memset(one_only[n][:, :, :, :], 0.0)
            last.then_inc(sm["rows_cleared"], 1)
            pool.wait_ge(sm["consts_set"], 1)
            pool.wait_ge(sm["rows_cleared"], 1)

            def rsqrt_of(b, mv_, r, eps_sem, pow_sem, done):
                nc.gpsimd.tensor_scalar(r[:, 0, :], mv_[:, :, 1], LN_EPS, None, ALU.add)
                nc.gpsimd.tensor_scalar(r[:, 2, :], mv_[:, :, 0], -1.0, None, ALU.mult).then_inc(sm[eps_sem], 1)
                wait(pool, sm[eps_sem], b, 1, 1, setup)
                nc.gpsimd.tensor_tensor(r[:, 1, :], r[:, 0, :], exponents[:, 0, :], ALU.pow).then_inc(sm[pow_sem], 1)
                wait(pool, sm[pow_sem], b, 1, 1, setup)
                nc.gpsimd.tensor_tensor(r[:, 3, :], r[:, 2, :], r[:, 1, :], ALU.mult).then_inc(sm[done], 1)

            def split(b, n, s):
                if s == 0:
                    wait(pool, sm[("q_copied", "k_copied")[n]], b, 1, 1, setup)
                    nc.gpsimd.tensor_tensor(parts[:, 1, n, :], qk[:, n, :], parts[:, 0, n, :], ALU.subtract
                                            ).then_inc(sm["mid_done"], 1)
                if s == 1:
                    wait(pool, sm["mid_done"], b, 2, n + 1, setup)
                    nc.gpsimd.tensor_tensor(qk[:, n, :], qk[:, n, :], parts[:, 0, n, :], ALU.subtract
                                            ).then_inc(sm["mid_left"], 1)
                if s == 2:
                    wait(pool, sm["mid_left"], b, 2, n + 1, setup)
                    nc.gpsimd.tensor_tensor(parts[:, 2, n, :], qk[:, n, :], parts[:, 1, n, :], ALU.subtract
                                            ).then_inc(sm["low_done"], 1)

            def body(i):
                post, fin, prep, ahead = i.plus(-1), i.plus(-2), i.plus(2), i.plus(1)
                for s in range(UNITS):
                    if has(i, "prepare"):
                        if s == 4:
                            wait(pool, sm["mv1_done"], prep, 1, 1, setup)
                            wait(pool, sm["xn_done"], prep, 1, 0, setup)
                            wait(pool, sm["valid_done"], prep, 1, 0, setup)
                            rsqrt_of(prep, mv1, rs1, "eps1_done", "pow1_done", "rs1_done")
                        for n, slots in enumerate(((15, 18, 20), (21, 24, 25))):
                            if s in slots:
                                split(prep, n, slots.index(s))
                    if has(i, "finish"):
                        if 1 <= s < 1 + FT:
                            f = s - 1
                            wait(pool, sm["gelu_done"], fin, 1, 1, setup)
                            wait(pool, sm["ssqf_ready"], fin, 1, 0, setup)
                            nc.gpsimd.tensor_tensor(h2[:, f, :], hT[:, f, :], hT[:, f, :], ALU.mult
                                                    ).then_inc(sm["h2_done"], 1)
                        if s == 9:
                            wait(pool, sm["ssq_copied"], fin, 1, 1, setup)
                            nc.gpsimd.tensor_scalar(rs_d[:, 0, :], ssq[:, :], 1.0 / (32 * FF), None, ALU.mult
                                                    ).then_inc(sm["msq_done"], 1)
                            wait(pool, sm["msq_done"], fin, 1, 1, setup)
                            nc.gpsimd.tensor_tensor(rs_d[:, 1, :], rs_d[:, 0, :], exponents[:, 1, :], ALU.pow
                                                    ).then_inc(sm["rmsh_done"], 1)
                        if s == 10:
                            wait(pool, sm["rmsh_done"], fin, 1, 1, setup)
                            nc.gpsimd.tensor_scalar(rs_d[:, 0, :], rs_d[:, 1, :], RMS_EPS, None, ALU.add
                                                    ).then_inc(sm["rmsh_eps"], 1)
                            wait(pool, sm["rmsh_eps"], fin, 1, 1, setup)
                            nc.gpsimd.tensor_tensor(rs_d[:, 2, :], rs_d[:, 0, :], exponents[:, 2, :], ALU.pow
                                                    ).then_inc(sm["invh_done"], 1)
                            wait(pool, sm["invh_done"], fin, 1, 1, setup)
                            nc.gpsimd.tensor_tensor(rs_d[:, 3, :], rs_d[:, 2, :], rs_d[:, 2, :], ALU.mult
                                                    ).then_inc(sm["sqh_done"], 1)
                        if s == 16:
                            wait(pool, sm["mvd"], fin, 1, 1, setup)
                            wait(pool, sm["sqh_done"], fin, 1, 1, setup)
                            nc.gpsimd.tensor_scalar(rs_d[:, 6, :], mv["d"][:, :, 0], -1.0, None, ALU.mult)
                            nc.gpsimd.tensor_tensor(rs_d[:, 0, :], rs_d[:, 3, :], mv["d"][:, :, 1], ALU.mult
                                                    ).then_inc(sm["vard_done"], 1)
                            wait(pool, sm["vard_done"], fin, 1, 1, setup)
                            nc.gpsimd.tensor_scalar(rs_d[:, 1, :], rs_d[:, 0, :], LN_EPS, None, ALU.add
                                                    ).then_inc(sm["epsd"], 1)
                            wait(pool, sm["epsd"], fin, 1, 1, setup)
                            nc.gpsimd.tensor_tensor(rs_d[:, 4, :], rs_d[:, 1, :], exponents[:, 0, :], ALU.pow
                                                    ).then_inc(sm["powd"], 1)
                        if s == 18:
                            wait(pool, sm["powd"], fin, 1, 1, setup)
                            nc.gpsimd.tensor_tensor(rs_d[:, 5, :], rs_d[:, 4, :], rs_d[:, 2, :], ALU.mult
                                                    ).then_inc(sm["scaled"], 1)
                            wait(pool, sm["scaled"], fin, 1, 1, setup)
                            nc.gpsimd.tensor_tensor(rs_d[:, 7, :], rs_d[:, 6, :], rs_d[:, 5, :], ALU.mult
                                                    ).then_inc(sm["rsd"], 1)
                        if s == 26:
                            wait(pool, sm["normd"], fin, 1, 1, setup)
                            wait(pool, sm["stored"], fin, DMA, 0, setup)
                            nc.gpsimd.tensor_tensor(o_sb[:, :, :], t_sb[:, :, :], y[fin.buf][:, :, :], ALU.add
                                                    ).then_inc(sm["o_done"], 1)
                    if has(i, "post"):
                        if s == 7:
                            wait(pool, sm["z_done"], post, 1, 1, setup)
                            wait(pool, sm["res_loaded"], post, 2 * DMA, 2 * DMA, setup)
                            wait(pool, sm["norma"], post, 1, 0, setup)
                            nc.gpsimd.tensor_tensor(x1[:, :, :], xn_res[:, :, :], z[:, :, :], ALU.add
                                                    ).then_inc(sm["x1_done"], 1)
                        if s == 11:
                            wait(pool, sm["mva"], post, 1, 1, setup)
                            rsqrt_of(post, mv["a"], rs["a"], "epsa", "powa", "rsa")
                        if s == 13:
                            wait(pool, sm["norma"], post, 1, 1, setup)
                            nc.gpsimd.tensor_tensor(a_out[:, :, :], a_out[:, :, :],
                                                    gamma_b[:, :].unsqueeze(1).broadcast_to([P, T, D]), ALU.mult
                                                    ).then_inc(sm["gam_done"], 1)
                        if s == 14:
                            wait(pool, sm["gam_done"], post, 1, 1, setup)
                            nc.gpsimd.tensor_tensor(a_out[:, :, :], a_out[:, :, :],
                                                    beta_b[:, :].unsqueeze(1).broadcast_to([P, T, D]), ALU.add
                                                    ).then_inc(sm["beta_done"], 1)
                        if s == 17:
                            wait(pool, sm["mvb"], post, 1, 1, setup)
                            rsqrt_of(post, mv["b"], rs["b"], "epsb", "powb", "rsb")
                        if s == 19:
                            wait(pool, sm["normb"], post, 1, 1, setup)
                            wait(pool, sm["o_done"], post, 1, -1, setup)
                            nc.gpsimd.tensor_tensor(y[post.buf][:, :, :], x_res[:, :, :], a_out[:, :, :], ALU.add
                                                    ).then_inc(sm["y_done"], 1)
                        r = rs["c"]
                        if s == 22:
                            wait(pool, sm["mvc"], post, 1, 1, setup)
                            nc.gpsimd.tensor_scalar(r[:, 0, :], mv["c"][:, :, 1], LN_EPS, None, ALU.add)
                            nc.gpsimd.tensor_scalar(r[:, 4, :], mv["c"][:, :, 0], -1.0, None, ALU.mult)
                            nc.gpsimd.tensor_scalar(r[:, 1, :], mv["c"][:, :, 1], 1.0, None, ALU.mult
                                                    ).then_inc(sm["epsc"], 1)
                            wait(pool, sm["epsc"], post, 1, 1, setup)
                            nc.gpsimd.tensor_tensor(r[:, 2:4, :], r[:, 0:2, :], exponents[:, 0:2, :], ALU.pow
                                                    ).then_inc(sm["powc"], 1)
                        if s == 23:
                            wait(pool, sm["powc"], post, 1, 1, setup)
                            nc.gpsimd.tensor_tensor(r[:, 0, :], r[:, 2, :], r[:, 3, :], ALU.mult
                                                    ).then_inc(sm["mulc"], 1)
                            wait(pool, sm["mulc"], post, 1, 1, setup)
                            nc.gpsimd.tensor_scalar(r[:, 1, :], r[:, 0, :], RMS_EPS, None, ALU.add
                                                    ).then_inc(sm["addc"], 1)
                            wait(pool, sm["addc"], post, 1, 1, setup)
                            nc.gpsimd.tensor_tensor(r[:, 0, :], r[:, 1, :], exponents[:, 2, :], ALU.pow
                                                    ).then_inc(sm["invc"], 1)
                            wait(pool, sm["invc"], post, 1, 1, setup)
                            nc.gpsimd.tensor_tensor(r[:, 3, :], r[:, 0, :], r[:, 2, :], ALU.mult
                                                    ).then_inc(sm["scalec"], 1)
                            wait(pool, sm["scalec"], post, 1, 1, setup)
                            nc.gpsimd.tensor_tensor(r[:, 5, :], r[:, 4, :], r[:, 3, :], ALU.mult
                                                    ).then_inc(sm["rsc"], 1)

                    if has(i, "attend"):
                        kt = (s // 2) % T
                        wait(pool, sm["exp_done"], i, UNITS, s + 1, setup)
                        wait(pool, sm["summed"], i, STEPS, s // 2 - RING // 2 + 1, setup)
                        nc.gpsimd.affine_select(out=diag[s % RING][:, :, :], in_=probs[s % RING][:, :, kt * P:(kt + 1) * P],
                                                compare_op=ALU.is_ge, fill=0.0, base=0, pattern=[[0, 2], [-1, P]],
                                                channel_multiplier=1).then_inc(sm["masked"], 1)

            turns(pool, body)


_INS = ["L0_attn_embedded", "L0_attn_Wq", "L0_attn_bq", "L0_attn_Wk", "L0_attn_bk", "L0_attn_Wv", "L0_attn_bv",
        "L0_attn_gamma", "L0_attn_beta", "L0_ffn_w_up", "L0_ffn_w_down"]


def kernel(**inputs):
    import concourse.bacc as bacc
    from concourse.bass_utils import run_bass_kernel_spmd

    nc = bacc.Bacc("TRN2", target_bir_lowering=False, num_devices=1)
    arrays, args = {}, []
    for name in _INS:
        a = np.ascontiguousarray(inputs[name])
        arrays[f"in_{name}_dram"] = a
        args.append(nc.dram_tensor(f"in_{name}_dram", a.shape, mybir.dt.from_np(a.dtype), kind="ExternalInput").ap())
    args.append(nc.dram_tensor("out_0_dram", (B, S, D), F32, kind="ExternalOutput").ap())
    build(nc, *args)
    r = run_bass_kernel_spmd(nc, [arrays], core_ids=[0])
    return r.results[0]["out_0_dram"]
```

```python
from contextlib import ExitStack

import numpy as np

import concourse.bass as bass
from concourse import mybir

F32 = mybir.dt.float32
BF16 = mybir.dt.bfloat16
ALU = mybir.AluOpType
ACT = mybir.ActivationFunctionType
AX_X = mybir.AxisListType.X

P = 128
B, S, D = 16, 512, 128
H, HD = 16, 8
FF = 512
T = S // P
FT = FF // P
PAIRS = H // 2
QUADS = H // 4
UNITS = PAIRS * T
STEPS = QUADS * T
LEAD = 24
LAG = 4
RING = 8
Q_PART = (0, 0, 1, 1, 0, 2)
K_PART = (0, 1, 0, 1, 2, 0)
ROWS = len(Q_PART) * HD
ROWS_ALL = 2 * ROWS
ROWS_M = ROWS_ALL + 4
INV_SQRT_S = float(1.0 / np.float32(np.sqrt(S)))
LN_EPS = 1e-5
XN_BOUND = 12.0
RMS_EPS = 1e-8
DMA = 16


class Turn:

    def __init__(self, offset, reg=None):
        self.offset, self.reg = offset, reg

    def plus(self, n):
        return Turn(self.offset + n, self.reg)

    @property
    def buf(self):
        return self.offset % 2

    @property
    def index(self):
        return self.offset if self.reg is None else self.reg * 2 + self.offset

    def count(self, per, n):
        c = per * self.offset + n
        return c if self.reg is None else self.reg * (2 * per) + c


def wait(eng, sem, turn, per, n, then=None):
    c = turn.count(per, n)
    if turn.reg is None and c < 1:
        return
    eng.wait_ge(sem, c)
    if then is not None and turn.reg is not None:
        eng.sem_inc(then, 1)


def build(nc, x, wq, bq, wk, bk, wv, bv, gamma, beta, w_up, w_down, out):
    with ExitStack() as ctx:
        def sb(name, shape, dt=F32):
            return ctx.enter_context(nc.sbuf_tensor(name, shape, dt))

        def sem(name):
            return ctx.enter_context(nc.semaphore(name))

        scoresT = [ctx.enter_context(nc.psum_tensor(f"scoresT{n}", [P, 2, S], F32)) for n in range(2)]
        scores = [ctx.enter_context(nc.psum_tensor(f"scores{n}", [P, S], F32)) for n in range(2)]
        sums = ctx.enter_context(nc.psum_tensor("sums", [P, S], F32))
        misc = ctx.enter_context(nc.psum_tensor("misc", [P, S], F32))
        sums_q = sums[:, :].rearrange("p (r a) -> p a r", a=S // 32)
        misc_t = misc[:, :].rearrange("p (t c) -> p t c", t=T)

        xn_dram = nc.dram_tensor("xn_dram", [B, S, D], F32).ap()
        part_dram = nc.dram_tensor("part_dram", [2, H, ROWS, S], BF16).ap()
        shift_dram = nc.dram_tensor("shift_dram", [2, 2, H // 2, S], BF16).ap()

        ident = sb("ident", [P, P])
        ident16 = sb("ident16", [P, P], BF16)
        ones = sb("ones", [P, P])
        exponents = sb("exponents", [P, 3, T])
        one_rows = sb("one_rows", [4, 2, S], BF16)
        w_nat = sb("w_nat", [P, 3, D])
        wT = sb("wT", [P, 3, D])
        bias = sb("bias", [P, 2])
        bv_b = sb("bv_b", [P, D])
        bv_v = sb("bv_v", [P, D])
        gamma_b = sb("gamma_b", [P, D])
        beta_b = sb("beta_b", [P, D])
        ff_abs = sb("ff_abs", [P, 2, 2])
        upT = sb("upT", [P, FF])
        downT = sb("downT", [P, FT, D])

        x_in = sb("x_in", [P, T, D])
        stat1 = sb("stat1", [P, T, 6])
        mv1 = sb("mv1", [P, T, 2])
        rs1 = sb("rs1", [P, 4, T])
        valid = [sb(f"valid{n}", [P, T]) for n in range(2)]
        xn = sb("xn", [P, T, D])
        xs = sb("xs", [P, T, D])
        xnT = sb("xnT", [P, S])
        qk = sb("qk", [P, 2, S])
        parts = sb("parts", [P, 3, 2, S], BF16)
        v_tok = sb("v_tok", [P, T, D])

        q_rows = [sb(f"q_rows{n}", [P, PAIRS, S], BF16) for n in range(2)]
        k_rows = [sb(f"k_rows{n}", [P, H, S], BF16) for n in range(2)]
        v_one = [sb(f"v_one{n}", [P, T, 2, 8, 32]) for n in range(2)]
        v_only = [sb(f"v_only{n}", [P, T, 2, 8, 32]) for n in range(2)]
        one_only = [sb(f"one_only{n}", [P, T, 2, 32]) for n in range(2)]
        neg_max = sb("neg_max", [P, H, T])
        shift = [sb(f"shift{g}", [P, 2, H // 2, T], BF16) for g in range(2)]
        shiftT = [sb(f"shiftT{g}", [2 * (H // 2) * T, P], BF16) for g in range(2)]
        probs = [sb(f"probs{n}", [P, 2, S]) for n in range(RING)]
        diag = [sb(f"diag{n}", [P, 2, P]) for n in range(RING)]
        sums_sb = [sb(f"sums_sb{g}", [P, S // 32, 32]) for g in range(2)]
        sums_t = [sb(f"sums_t{g}", [P, S // 32, 2, 16]) for g in range(2)]

        neg = sb("neg", [P, T, D])
        x_res = sb("x_res", [P, T, D])
        xn_res = sb("xn_res", [P, T, D])
        inv_den = sb("inv_den", [P, S // 32, 2])
        z = sb("z", [P, T, D])
        x1 = sb("x1", [P, T, D])
        a_out = sb("a_out", [P, T, D])
        y = [sb(f"y{n}", [P, T, D]) for n in range(2)]
        xr = sb("xr", [P, T, D])
        stat = {n: sb(f"stat_{n}", [P, T, 6]) for n in "abcd"}
        mv = {n: sb(f"mv_{n}", [P, T, 2]) for n in "abcd"}
        rs = {n: sb(f"rs_{n}", [P, 6, T]) for n in "abc"}
        xrT = sb("xrT", [P, S])
        up_sb = sb("up_sb", [P, FT, S])
        hT = sb("hT", [P, FT, S])
        h2 = up_sb
        ff_nat = hT[:, 0:2, :]
        ff_pos, ff_neg = up_sb[:, 0, :], up_sb[:, 1, :]
        ssqf = sb("ssqf", [P, S])
        ssq = sb("ssq", [P, T])
        rs_d = sb("rs_d", [P, 8, T])
        t_sb = sb("t_sb", [P, T, D])
        o_sb = sb("o_sb", [P, T, D])

        names = """weights_in ff_in consts_set ident_set ident_made ones_made one_rows_set one_rows_made one_rows_in
            k_zeroed values_zeroed w_transposed w_copied bv_done abs_done abs_summed thr_done neg_done
            tern_done diff_done ternary_done ffT_done ffT_copied""".split()
        names += """x_loaded stat1_done mv1_done eps1_done pow1_done rs1_done xn_done valid_done xs_done
            xn_stored xnT_ready xnT_copied q_ready q_copied k_ready k_copied v_ready v_added v_done
            v_placed mid_done mid_left low_done parts_stored rows_loaded""".split()
        names += """scoresT_ready exp_done masked summed sums_copied scores_ready max_done
            shift_hi shift_lo shift_ready shift_copied shift_stored shift_loaded""".split()
        names += """res_loaded sumsT_done inv_done z_scaled zneg_done z_done x1_done
            stata mva epsa powa rsa norma gam_done beta_done statb mvb epsb powb rsb normb y_done
            statc mvc epsc powc mulc addc invc scalec rsc xr_done xrT_ready xrT_copied up_ready up_copied gelu_done
            h2_done ssqf_ready ssqf_copied ssq_ready ssq_copied msq_done rmsh_done rmsh_eps invh_done sqh_done
            t_ready t_copied statd mvd vard_done epsd powd scaled rsd normd o_done stored""".split()
        sm = {n: sem("s_" + n) for n in names}
        setup = sm["values_zeroed"]

        def to_rows(src, n):
            return src.rearrange("(o n) -> o n", o=1).broadcast_to([P, n])

        block = ctx.enter_context(nc.Block())

        def turns(eng, body):
            for i in range(-2, 3):
                body(Turn(i))
            with eng.Fori(1, (B - 4) // 2) as k:
                for u in (1, 2):
                    body(Turn(u, k))
            for i in range(B - 3, B + 2):
                body(Turn(i))

        def has(turn, what):
            if turn.reg is not None:
                return True
            i = turn.offset
            return {"attend": 0 <= i < B, "ahead": 0 <= i + 1 < B, "prepare": 0 <= i + 2 < B,
                    "post": 0 <= i - 1 < B, "finish": 0 <= i - 2 < B}[what]

        def units_of_max(turn, s):
            u = s + LEAD
            if u < UNITS:
                return (turn, u) if has(turn, "attend") else None
            return (turn.plus(1), u - UNITS) if has(turn, "ahead") else None

        def early(b, u):
            return b.reg is None and b.offset == 0 and u < LEAD

        def max_bank(b, u, hp):
            return scoresT[1][:, hp, :] if early(b, u) and u % 2 else scores[hp][:, :]

        def step_of(turn, s):
            w, half = (s - LAG) // 2, s % 2
            if w < 0:
                return (turn.plus(-1), w + STEPS, half) if has(turn, "post") else None
            return (turn, w, half) if has(turn, "attend") else None

        @block.sync
        def _(sp):
            sp.dma_start(x_in[:, :, :], x[0].rearrange("(t p) d -> p t d", p=P)).then_inc(sm["x_loaded"], DMA)
            for n, w in enumerate((wq, wk, wv)):
                sp.dma_start(w_nat[:, n, :], w).then_inc(sm["weights_in"], DMA)
            for n, v in enumerate((bq, bk)):
                sp.dma_start(bias[:, n:n + 1], v.rearrange("(d o) -> d o", o=1)).then_inc(sm["weights_in"], DMA)
            for dst, v in ((bv_b, bv), (gamma_b, gamma), (beta_b, beta)):
                sp.dma_start(dst[:, :], to_rows(v, D)).then_inc(sm["weights_in"], DMA)
            sp.dma_start(ff_nat[:, 0, :].rearrange("p (t d) -> p t d", t=FT),
                         w_up.rearrange("(t p) d -> p t d", p=P)).then_inc(sm["ff_in"], DMA)
            sp.dma_start(ff_nat[:, 1, :], w_down).then_inc(sm["ff_in"], DMA)
            sp.wait_ge(sm["one_rows_made"], 1)
            for n in range(2):
                for pair in range(PAIRS):
                    sp.dma_start(k_rows[n][ROWS_ALL:ROWS_M, 2 * pair:2 * pair + 2, :], one_rows[:, :, :]
                                 ).then_inc(sm["one_rows_in"], DMA)

            def shift_out(b, g):
                wait(sp, sm["shift_copied"], b, 2, g + 1, setup)
                wait(sp, sm["shift_loaded"], b, 4 * DMA, 2 * DMA * (g - 1), setup)
                sp.dma_start(shift_dram[g].rearrange("c h (t q) -> (c h t) q", t=T),
                             shiftT[g][:, :]).then_inc(sm["shift_stored"], DMA)
                wait(sp, sm["shift_stored"], b, 2 * DMA, DMA * (g + 1), setup)
                for hp in range(2):
                    r = ROWS_ALL + 2 * hp
                    sp.dma_start(q_rows[b.buf][r:r + 2, 4 * g:4 * g + 4, :],
                                 shift_dram[g].rearrange("c (r hp) q -> hp c r q", hp=2)[hp]
                                 ).then_inc(sm["shift_loaded"], DMA)

            def parts_out(b, which, part_of):
                wait(sp, sm["low_done"], b, 2, which + 1, setup)
                for slot, part in enumerate(part_of):
                    sp.dma_start(part_dram[which, :, HD * slot:HD * slot + HD, :],
                                 parts[:, part, which, :]).then_inc(sm["parts_stored"], DMA)

            def body(i):
                post, fin, prep = i.plus(-1), i.plus(-2), i.plus(2)
                if has(i, "post"):
                    wait(sp, sm["y_done"], post, 1, 0, setup)
                    wait(sp, sm["xn_stored"], post, DMA, DMA, setup)
                    sp.dma_start(x_res[:, :, :], x[post.index].rearrange("(t p) d -> p t d", p=P)
                                 ).then_inc(sm["res_loaded"], DMA)
                    sp.dma_start(xn_res[:, :, :], xn_dram[post.index].rearrange("(t p) d -> p t d", p=P)
                                 ).then_inc(sm["res_loaded"], DMA)
                if has(i, "prepare"):
                    wait(sp, sm["xn_done"], prep, 1, 1, setup)
                    sp.dma_start(xn_dram[prep.index].rearrange("(t p) d -> p t d", p=P),
                                 xn[:, :, :]).then_inc(sm["xn_stored"], DMA)
                    if has(i.plus(1), "prepare"):
                        sp.dma_start(x_in[:, :, :], x[prep.plus(1).index].rearrange("(t p) d -> p t d", p=P)
                                     ).then_inc(sm["x_loaded"], DMA)
                if has(i, "attend"):
                    shift_out(i, 1)
                if has(i, "prepare"):
                    wait(sp, sm["rows_loaded"], prep, 4 * DMA, 0, setup)
                    parts_out(prep, 0, Q_PART)
                if has(i, "ahead"):
                    shift_out(i.plus(1), 0)
                if has(i, "prepare"):
                    parts_out(prep, 1, K_PART)
                if has(i, "finish"):
                    wait(sp, sm["o_done"], fin, 1, 1, setup)
                    sp.dma_start(out[fin.index].rearrange("(t p) d -> p t d", p=P),
                                 o_sb[:, :, :]).then_inc(sm["stored"], DMA)
                if has(i, "prepare"):
                    wait(sp, sm["parts_stored"], prep, 12 * DMA, 12 * DMA, setup)
                    wait(sp, sm["scoresT_ready"], i, UNITS, UNITS, setup)
                    if prep.reg is None and prep.offset < 2:
                        sp.wait_ge(sm["k_zeroed"], prep.offset + 1)
                    for which, rows in ((0, q_rows), (1, k_rows)):
                        for hp in range(2):
                            dst = rows[prep.buf][ROWS * hp:ROWS * hp + ROWS, :, :]
                            if which:
                                dst = dst.rearrange("k (r hp) q -> k hp r q", hp=2)[:, hp]
                            sp.dma_start(dst,
                                         part_dram[which].rearrange("(r hp) k q -> hp k r q", hp=2)[hp]
                                         ).then_inc(sm["rows_loaded"], DMA)

            turns(sp, body)
            sp.wait_ge(sm["stored"], DMA * B)
            sp.wait_ge(sm["xn_stored"], DMA * B)

        @block.tensor
        def _(pe):
            reads = []

            def take_misc(reader):
                if reads:
                    wait(pe, *reads[-1])
                reads.append(reader)

            pe.wait_ge(sm["weights_in"], 8 * DMA)
            pe.wait_ge(sm["ident_made"], 2)
            for n in range(3):
                last = nc.tensor.transpose(misc[:, n * P:(n + 1) * P], w_nat[:, n, :], ident[:, :])
            last.then_inc(sm["w_transposed"], 1)
            pe.wait_ge(sm["w_copied"], 1)

            def setup_ff():
                pe.wait_ge(sm["ones_made"], 1)
                pe.wait_ge(sm["abs_done"], 1)
                nc.tensor.matmul(sums[:, 0:2], ones[:, :], ff_abs[:, 0, :], start=True, stop=True
                                 ).then_inc(sm["abs_summed"], 1)
                pe.wait_ge(sm["ternary_done"], 2)
                for n in range(2):
                    for t in range(FT):
                        last = nc.tensor.transpose(scoresT[0][:, n, t * P:(t + 1) * P],
                                                   ff_nat[:, n, t * P:(t + 1) * P], ident[:, :])
                last.then_inc(sm["ffT_done"], 1)

            def score_unit(b, s):
                pair, kt = 2 * (s // 8) + s % 2, (s // 2) % T
                if s == 0 and b.reg is None and b.offset == 0:
                    pe.wait_ge(sm["ffT_copied"], 1)
                    pe.wait_ge(sm["one_rows_in"], DMA * 2 * PAIRS)
                    wait(pe, sm["max_done"], b, 2 * UNITS, 2 * LEAD)
                if s % 16 == 0:
                    wait(pe, sm["shift_loaded"], b, 4 * DMA, 2 * DMA * (s // 16 + 1))
                wait(pe, sm["exp_done"], b, UNITS, s - 1)
                for hp in range(2):
                    h = 2 * pair + hp
                    last = nc.tensor.matmul(scoresT[s % 2][:, hp, :], k_rows[b.buf][0:ROWS_M, h, kt * P:(kt + 1) * P],
                                            q_rows[b.buf][0:ROWS_M, pair, :], start=True, stop=True)
                last.then_inc(sm["scoresT_ready"], 1)

            def max_unit(b, u, hp):
                pair, qt = u // T, u % T
                if u == 0 and hp == 0:
                    wait(pe, sm["rows_loaded"], b, 4 * DMA, 4 * DMA)
                if early(b, u):
                    if u == 1 and hp == 0:
                        pe.wait_ge(sm["ffT_copied"], 1)
                    wait(pe, sm["max_done"], b, 2 * UNITS, 2 * u - 3 + hp)
                else:
                    wait(pe, sm["max_done"], b, 2 * UNITS, 2 * u - 1 + hp)
                nc.tensor.matmul(max_bank(b, u, hp), q_rows[b.buf][0:ROWS_ALL, pair, qt * P:(qt + 1) * P],
                                 k_rows[b.buf][0:ROWS_ALL, 2 * pair + hp, :], start=True, stop=True
                                 ).then_inc(sm["scores_ready"], 1)

            def sum_step(b, w, half):
                quad, kt = w // T, w % T
                i, g = quad % 2, quad // 2
                n = (2 * w) % RING
                first, final = i == 0 and kt == 0, i == 1 and kt == T - 1
                if half == 0:
                    if kt == 0 and g == 0:
                        wait(pe, sm["v_placed"], b, 2, i + 1)
                    if first:
                        wait(pe, sm["sums_copied"], b, 2, g)
                    wait(pe, sm["masked"], b, UNITS, 2 * w + 2)
                    for j in range(4):
                        nc.tensor.matmul(sums[32 * j:32 * j + 32, kt * P:], one_only[b.buf][:, kt, i, :],
                                         probs[n + j // 2][:, j % 2, kt * P:], start=first, stop=False)
                if half == (kt < T - 1):
                    for j in range(4):
                        last = nc.tensor.matmul(sums[32 * j:32 * j + 32, kt * P:(kt + 1) * P],
                                                v_only[b.buf][:, kt, i, 4 * g + j, :], diag[n + j // 2][:, j % 2, :],
                                                start=False, stop=False)
                if half == 1:
                    if kt:
                        for j in range(4):
                            last = nc.tensor.matmul(sums[32 * j:32 * j + 32, 0:kt * P], v_one[b.buf][:, kt, i, 4 * g + j, :],
                                                    probs[n + j // 2][:, j % 2, 0:kt * P], start=False, stop=final)
                    last.then_inc(sm["summed"], 1)

            def transpose4(src, ready):
                for t in range(T):
                    last = nc.tensor.transpose(misc_t[:, t, :], src(t), ident[:, :])
                last.then_inc(sm[ready], 1)

            def shift_transpose(b, g):
                take_misc((sm["shift_copied"], b, 2, g + 1))
                wait(pe, sm["shift_lo"], b, 2, g + 1, setup)
                nc.tensor.transpose(misc[0:64, 0:64].bitcast(BF16), shift[g][:, :, :, :].rearrange(
                    "p c h t -> p (c h t)"), ident16[:, :]).then_inc(sm["shift_ready"], 1)

            def body(i):
                post, fin, prep = i.plus(-1), i.plus(-2), i.plus(2)
                reads.clear()
                if has(i.plus(-1), "post"):
                    reads.append((sm["up_copied"], i.plus(-2), FT, FT) if has(i.plus(-1), "attend")
                                 else (sm["xrT_copied"], i.plus(-2), 1, 1))
                elif has(i.plus(-1), "ahead"):
                    reads.append((sm["shift_copied"], i, 2, 1))
                elif has(i.plus(-1), "prepare"):
                    reads.append((sm["k_copied"], i.plus(1), 1, 1))
                for s in range(UNITS):
                    if units_of_max(i, s):
                        max_unit(*units_of_max(i, s), 0)
                    late = s % 16 == LAG
                    if step_of(i, s) and not late:
                        sum_step(*step_of(i, s))
                    if units_of_max(i, s):
                        max_unit(*units_of_max(i, s), 1)
                    if has(i, "ahead") and s == 0:
                        take_misc((sm["v_added"], i.plus(1), 1, 1))
                        wait(pe, sm["xnT_copied"], i.plus(1), 1, 1)
                        for t in range(T):
                            last = nc.tensor.matmul(misc_t[:, t, :], xnT[:, t * P:(t + 1) * P], wT[:, 2, :],
                                                    start=True, stop=True)
                        last.then_inc(sm["v_ready"], 1)
                    if has(i, "finish"):
                        for t in {1: (0, 1), 3: (2,), 5: (3,)}.get(s, ()):
                            if t == 0:
                                take_misc((sm["t_copied"], fin, 1, 1))
                                wait(pe, sm["gelu_done"], fin, 1, 1)
                            for f in range(FT):
                                last = nc.tensor.matmul(misc_t[:, t, :], hT[:, f, t * P:(t + 1) * P],
                                                        downT[:, f, :], start=f == 0, stop=f == FT - 1)
                            if t == T - 1:
                                last.then_inc(sm["t_ready"], 1)
                        if s == 7:
                            take_misc((sm["ssqf_copied"], fin, 1, 1))
                            wait(pe, sm["h2_done"], fin, FT, FT)
                            for f in range(FT):
                                last = nc.tensor.matmul(misc[32 * f:32 * f + 32, :], ones[:, 0:32], h2[:, f, :],
                                                        start=True, stop=True)
                            last.then_inc(sm["ssqf_ready"], 1)
                        if s == 8:
                            take_misc((sm["ssq_copied"], fin, 1, 1))
                            wait(pe, sm["ssqf_copied"], fin, 1, 1)
                            for t in range(T):
                                last = nc.tensor.matmul(misc[:, t:t + 1], ssqf[:, t * P:(t + 1) * P], ones[:, 0:1],
                                                        start=True, stop=True)
                            last.then_inc(sm["ssq_ready"], 1)
                    if s == 9 and has(i, "attend"):
                        shift_transpose(i, 1)
                    if s == 25 and has(i, "ahead"):
                        shift_transpose(i.plus(1), 0)
                    if has(i, "post"):
                        if 27 <= s < 27 + FT:
                            f = s - 27
                            to = scoresT[f // 2][:, f % 2, :]
                            if has(i, "attend"):
                                take_misc((sm["up_copied"], post, FT, f + 1))
                                to = misc[:, :]
                            if f == 0:
                                wait(pe, sm["exp_done"], post, UNITS, UNITS)
                                wait(pe, sm["xrT_copied"], post, 1, 1)
                            nc.tensor.matmul(to, upT[:, f * P:(f + 1) * P], xrT[:, :],
                                             start=True, stop=True).then_inc(sm["up_ready"], 1)
                    if has(i, "prepare"):
                        if s == 10:
                            take_misc((sm["xnT_copied"], prep, 1, 1))
                            wait(pe, sm["xs_done"], prep, 1, 1)
                            transpose4(lambda t: xs[:, t, :], "xnT_ready")
                        if s == 13:
                            take_misc((sm["q_copied"], prep, 1, 1))
                            wait(pe, sm["xnT_copied"], prep, 1, 1)
                            nc.tensor.matmul(misc[:, :], wT[:, 0, :], xnT[:, :], start=True, stop=True
                                             ).then_inc(sm["q_ready"], 1)
                        if s == 15:
                            take_misc((sm["k_copied"], prep, 1, 1))
                            nc.tensor.matmul(misc[:, :], wT[:, 1, :], xnT[:, :], start=True, stop=True
                                             ).then_inc(sm["k_ready"], 1)
                        if s == 31 and prep.reg is None and prep.offset == 0:
                            setup_ff()
                    if has(i, "attend"):
                        score_unit(i, s)
                    if step_of(i, s) and late:
                        sum_step(*step_of(i, s))
                    if has(i, "post") and s == 26:
                        take_misc((sm["xrT_copied"], post, 1, 1))
                        wait(pe, sm["xr_done"], post, 1, 1)
                        transpose4(lambda t: xr[:, t, :], "xrT_ready")

            turns(pe, body)

        @block.scalar
        def _(act):
            act.wait_ge(sm["w_transposed"], 1)
            nc.scalar.copy(wT[:, 0:2, :], misc[:, 0:2 * P].rearrange("p (n d) -> p n d", n=2))
            nc.scalar.copy(wT[:, 2, :].rearrange("p (i g c) -> p g i c", i=2, g=2),
                           misc[:, 2 * P:3 * P].rearrange("p (g i c) -> p g i c", i=2, g=2)
                           ).then_inc(sm["w_copied"], 1)
            act.wait_ge(sm["weights_in"], 8 * DMA)
            nc.scalar.copy(bv_v[:, :].rearrange("p (i g c) -> p g i c", i=2, g=2),
                           bv_b[:, :].rearrange("p (g i c) -> p g i c", i=2, g=2)).then_inc(sm["bv_done"], 1)

            def setup_ff():
                act.wait_ge(sm["ffT_done"], 1)
                nc.scalar.copy(upT[:, :], scoresT[0][:, 0, :])
                nc.scalar.copy(downT[:, :, :], scoresT[0][:, 1, :].rearrange("p (t d) -> p t d", t=FT)
                               ).then_inc(sm["ffT_copied"], 1)

            def normalise(dst, src, scale, minus_mean_scale, done):
                for t in range(T):
                    last = nc.scalar.activation(dst[:, t, :], src[:, t, :], ACT.Identity,
                                                bias=minus_mean_scale[:, t:t + 1], scale=scale[:, t:t + 1])
                last.then_inc(sm[done], 1)

            def body(i):
                post, fin, prep, ahead = i.plus(-1), i.plus(-2), i.plus(2), i.plus(1)
                for s in range(UNITS):
                    if s == 19 and has(i, "attend"):
                        wait(act, sm["summed"], i, STEPS, STEPS // 2)
                        wait(act, sm["sumsT_done"], i, 2, 0)
                        nc.scalar.copy(sums_sb[0][:, :, :], sums_q).then_inc(sm["sums_copied"], 1)
                    if has(i, "finish"):
                        if s == 6:
                            wait(act, sm["t_ready"], fin, 1, 1)
                            wait(act, sm["o_done"], fin, 1, 0)
                            nc.scalar.copy(t_sb[:, :, :], misc_t).then_inc(sm["t_copied"], 1)
                        if s == 7:
                            wait(act, sm["ssqf_ready"], fin, 1, 1)
                            wait(act, sm["ssq_ready"], fin, 1, 0)
                            nc.scalar.copy(ssqf[:, :], misc[:, :]).then_inc(sm["ssqf_copied"], 1)
                        if s == 22:
                            wait(act, sm["rsd"], fin, 1, 1)
                            normalise(t_sb, t_sb, rs_d[:, 5, :], rs_d[:, 7, :], "normd")
                    if has(i, "post"):
                        if s == 3:
                            wait(act, sm["summed"], post, STEPS, STEPS)
                            wait(act, sm["sumsT_done"], post, 2, 0)
                            nc.scalar.copy(sums_sb[1][:, :, :], sums_q).then_inc(sm["sums_copied"], 1)
                        if s == 11:
                            wait(act, sm["rsa"], post, 1, 1)
                            wait(act, sm["y_done"], post, 1, 0)
                            normalise(a_out, x1, rs["a"][:, 1, :], rs["a"][:, 3, :], "norma")
                        if s == 17:
                            wait(act, sm["rsb"], post, 1, 1)
                            normalise(a_out, a_out, rs["b"][:, 1, :], rs["b"][:, 3, :], "normb")
                        if s == 24:
                            wait(act, sm["rsc"], post, 1, 1)
                            wait(act, sm["xrT_ready"], post, 1, 0)
                            normalise(xr, y[post.buf], rs["c"][:, 3, :], rs["c"][:, 5, :], "xr_done")
                        if s == 26:
                            wait(act, sm["xrT_ready"], post, 1, 1)
                            wait(act, sm["up_ready"], post, FT, 0)
                            nc.scalar.copy(xrT[:, :], misc[:, :]).then_inc(sm["xrT_copied"], 1)
                        if 27 <= s < 27 + FT and has(i, "attend"):
                            f = s - 27
                            wait(act, sm["up_ready"], post, FT, f + 1)
                            wait(act, sm["ssqf_ready"], post, 1, 0)
                            nc.scalar.copy(up_sb[:, f, :], misc[:, :]).then_inc(sm["up_copied"], 1)
                        if s == 31:
                            wait(act, sm["t_ready"], post, 1, 0)
                            wait(act, sm["h2_done"], post, FT, 0)
                            if has(i, "attend"):
                                wait(act, sm["up_copied"], post, FT, FT)
                                nc.scalar.activation(hT[:, :, :], up_sb[:, :, :], ACT.Gelu
                                                     ).then_inc(sm["gelu_done"], 1)
                            else:
                                wait(act, sm["up_ready"], post, FT, FT // 2)
                                nc.scalar.activation(hT[:, 0:2, :], scoresT[0][:, :, :], ACT.Gelu)
                                wait(act, sm["up_ready"], post, FT, FT)
                                nc.scalar.activation(hT[:, 2:4, :], scoresT[1][:, :, :], ACT.Gelu
                                                     ).then_inc(sm["gelu_done"], 1)
                    if has(i, "attend") and s in (2, 5):
                        i2 = s // 5
                        c = 16 * i2
                        wait(act, sm["v_done"], i, 1, 1)
                        nc.scalar.copy(v_one[i.buf][:, :, i2, :, c:c + HD],
                                       v_only[i.buf][:, :, i2, :, c:c + HD])
                        nc.scalar.copy(v_one[i.buf][:, :, i2, :, c + HD:c + 2 * HD],
                                       valid[i.buf][:, :].unsqueeze(2).unsqueeze(3).broadcast_to([P, T, 8, HD]))
                        nc.scalar.copy(one_only[i.buf][:, :, i2, c + HD:c + 2 * HD],
                                       valid[i.buf][:, :].unsqueeze(2).broadcast_to([P, T, HD])).then_inc(sm["v_placed"], 1)
                    if has(i, "prepare"):
                        if s == 6:
                            wait(act, sm["rs1_done"], prep, 1, 1)
                            wait(act, sm["xn_stored"], prep, DMA, 0)
                            wait(act, sm["xs_done"], prep, 1, 0)
                            normalise(xn, x_in, rs1[:, 1, :], rs1[:, 3, :], "xn_done")
                        if s == 10:
                            wait(act, sm["xnT_ready"], prep, 1, 1)
                            wait(act, sm["v_ready"], prep, 1, 0)
                            nc.scalar.copy(xnT[:, :], misc[:, :]).then_inc(sm["xnT_copied"], 1)
                        for at, which, n in ((13, "q", 0), (15, "k", 1)):
                            if s == at:
                                wait(act, sm[which + "_ready"], prep, 1, 1)
                                wait(act, sm["low_done"], prep, 2, n - 1)
                                wait(act, sm["parts_stored"], prep, 12 * DMA, 0)
                                nc.scalar.activation(qk[:, n, :], misc[:, :], ACT.Identity, bias=bias[:, n:n + 1],
                                                     scale=1.0)
                                nc.scalar.activation(parts[:, 0, n, :], misc[:, :], ACT.Identity, bias=bias[:, n:n + 1],
                                                     scale=1.0).then_inc(sm[which + "_copied"], 1)
                        if s == 31 and prep.reg is None and prep.offset == 0:
                            setup_ff()
                    for at, g, b, part in ((9, 1, i, "attend"), (25, 0, i.plus(1), "ahead")):
                        if s == at and has(i, part):
                            wait(act, sm["shift_ready"], b, 2, g + 1)
                            wait(act, sm["shift_stored"], b, 2 * DMA, DMA * (g - 1))
                            nc.scalar.copy(shiftT[g][:, :], misc[0:64, 0:64].bitcast(BF16)
                                           ).then_inc(sm["shift_copied"], 1)

                    if has(i, "attend"):
                        wait(act, sm["scoresT_ready"], i, UNITS, s + 1)
                        wait(act, sm["summed"], i, STEPS, s // 2 - RING // 2 + 1)
                        nc.scalar.activation(probs[s % RING][:, :, :], scoresT[s % 2][:, :, :], ACT.Exp,
                                             scale=INV_SQRT_S).then_inc(sm["exp_done"], 1)

            turns(act, body)

        @block.vector
        def _(dve):
            def setup_rows():
                for n in range(2):
                    nc.vector.memset(k_rows[n][0:ROWS_ALL, :, :].bitcast(F32), 0.0).then_inc(sm["k_zeroed"], 1)

            def setup_ff():
                dve.wait_ge(sm["ff_in"], 2 * DMA)
                for n in range(2):
                    last = nc.vector.tensor_reduce(ff_abs[:, 0, n:n + 1], ff_nat[:, n, :], AX_X, ALU.add,
                                                   apply_absolute_value=True)
                last.then_inc(sm["abs_done"], 1)
                dve.wait_ge(sm["abs_summed"], 1)
                nc.vector.tensor_scalar(ff_abs[:, 1, :], sums[:, 0:2], 1.0 / (FF * D), 0.5, ALU.mult, ALU.mult
                                        ).then_inc(sm["thr_done"], 1)
                dve.wait_ge(sm["thr_done"], 1)
                nc.vector.tensor_scalar(ff_abs[:, 0, :], ff_abs[:, 1, :], -1.0, None, ALU.mult
                                        ).then_inc(sm["thr_done"], 1)
                dve.wait_ge(sm["thr_done"], 2)
                for n in range(2):
                    nc.vector.tensor_scalar(ff_pos, ff_nat[:, n, :], ff_abs[:, 1, n:n + 1], None, ALU.is_gt)
                    nc.vector.tensor_scalar(ff_neg, ff_nat[:, n, :], ff_abs[:, 0, n:n + 1], None, ALU.is_lt
                                            ).then_inc(sm["neg_done"], 1)
                    dve.wait_ge(sm["neg_done"], n + 1)
                    nc.vector.tensor_tensor(ff_pos, ff_pos, ff_neg, ALU.subtract
                                            ).then_inc(sm["tern_done"], 1)
                    dve.wait_ge(sm["tern_done"], n + 1)
                    nc.vector.tensor_tensor(ff_neg, ff_pos, ff_nat[:, n, :], ALU.subtract
                                            ).then_inc(sm["diff_done"], 1)
                    dve.wait_ge(sm["diff_done"], n + 1)
                    nc.vector.tensor_tensor(ff_nat[:, n, :], ff_nat[:, n, :], ff_neg, ALU.add
                                            ).then_inc(sm["ternary_done"], 1)
                    dve.wait_ge(sm["ternary_done"], n + 1)

            def statistics(b, src, st, mv_, st_sem, mv_sem, half):
                if half == 0:
                    for t in range(T):
                        last = nc.vector.bn_stats(st[:, t, :], src[:, t, :])
                    last.then_inc(sm[st_sem], 1)
                    return
                wait(dve, sm[st_sem], b, 1, 1, setup)
                for t in range(T):
                    last = nc.vector.bn_aggr(mv_[:, t, :], st[:, t, :])
                last.then_inc(sm[mv_sem], 1)

            def quotient(b, g, half):
                if half == 0:
                    wait(dve, sm["sums_copied"], b, 2, g + 1)
                    nc.vector.transpose(sums_t[g][:, :, :, :].rearrange("p a i c -> p (a i c)"),
                                        sums_sb[g][:, :, :].rearrange("p a r -> p (a r)")
                                        ).then_inc(sm["sumsT_done"], 1)
                    return
                wait(dve, sm["sumsT_done"], b, 2, g + 1)
                nc.vector.reciprocal(inv_den[:, :, :], sums_t[g][:, :, :, HD]).then_inc(sm["inv_done"], 1)
                wait(dve, sm["x1_done"], b, 1, 0)
                wait(dve, sm["inv_done"], b, 2, g + 1)
                for i2 in range(2):
                    last = nc.vector.tensor_tensor(
                        z[:, 2 * g + i2, :].rearrange("p (a c) -> p a c", c=HD), sums_t[g][:, :, i2, 0:HD],
                        inv_den[:, :, i2].unsqueeze(2).broadcast_to([P, S // 32, HD]), ALU.mult)
                last.then_inc(sm["z_scaled"], 1)

            def split_shift(b, g):
                wait(dve, sm["max_done"], b, 2 * UNITS, UNITS * (g + 1))
                wait(dve, sm["shift_ready"], b, 2, g - 1)
                nc.vector.tensor_copy(shift[g][:, 0], neg_max[:, 8 * g:8 * g + 8, :]).then_inc(sm["shift_hi"], 1)
                wait(dve, sm["shift_hi"], b, 2, g + 1)
                nc.vector.tensor_tensor(shift[g][:, 1], neg_max[:, 8 * g:8 * g + 8, :], shift[g][:, 0],
                                        ALU.subtract).then_inc(sm["shift_lo"], 1)
                wait(dve, sm["shift_lo"], b, 2, g + 1)

            def last_turns(i, s):
                post, fin = i.plus(-1), i.plus(-2)
                if has(i, "post"):
                    if s == 7:
                        wait(dve, sm["z_done"], post, 1, 1)
                        wait(dve, sm["res_loaded"], post, 2 * DMA, 2 * DMA)
                        wait(dve, sm["norma"], post, 1, 0)
                        nc.vector.tensor_tensor(x1[:, :, :], xn_res[:, :, :], z[:, :, :], ALU.add
                                                ).then_inc(sm["x1_done"], 1)
                    if s == 12:
                        wait(dve, sm["norma"], post, 1, 1)
                        nc.vector.tensor_tensor(a_out[:, :, :], a_out[:, :, :],
                                                gamma_b[:, :].unsqueeze(1).broadcast_to([P, T, D]), ALU.mult
                                                ).then_inc(sm["gam_done"], 1)
                    if s == 13:
                        wait(dve, sm["gam_done"], post, 1, 1)
                        nc.vector.tensor_tensor(a_out[:, :, :], a_out[:, :, :],
                                                beta_b[:, :].unsqueeze(1).broadcast_to([P, T, D]), ALU.add
                                                ).then_inc(sm["beta_done"], 1)
                    if s == 18:
                        wait(dve, sm["normb"], post, 1, 1)
                        wait(dve, sm["o_done"], post, 1, -1)
                        nc.vector.tensor_tensor(y[post.buf][:, :, :], x_res[:, :, :], a_out[:, :, :], ALU.add
                                                ).then_inc(sm["y_done"], 1)
                if has(i, "finish"):
                    if s in (1, 2):
                        wait(dve, sm["gelu_done"], fin, 1, 1)
                        wait(dve, sm["ssqf_ready"], fin, 1, 0)
                        nc.vector.tensor_tensor(h2[:, s + 1, :], hT[:, s + 1, :], hT[:, s + 1, :], ALU.mult
                                                ).then_inc(sm["h2_done"], 1)
                    if s == 29:
                        wait(dve, sm["normd"], fin, 1, 1)
                        wait(dve, sm["stored"], fin, DMA, 0)
                        nc.vector.tensor_tensor(o_sb[:, :, :], t_sb[:, :, :], y[fin.buf][:, :, :], ALU.add
                                                ).then_inc(sm["o_done"], 1)

            def body(i):
                post, fin, prep, ahead = i.plus(-1), i.plus(-2), i.plus(2), i.plus(1)
                for s in range(UNITS):
                    if units_of_max(i, s):
                        b, u = units_of_max(i, s)
                        for hp in range(2):
                            wait(dve, sm["scores_ready"], b, 2 * UNITS, 2 * u + hp + 1)
                            nc.vector.tensor_reduce(neg_max[:, 2 * (u // T) + hp, u % T:u % T + 1], max_bank(b, u, hp),
                                                    AX_X, ALU.max, negate=True).then_inc(sm["max_done"], 1)
                    if s == 8 and has(i, "attend"):
                        split_shift(i, 1)
                    if s == 24 and has(i, "ahead"):
                        split_shift(ahead, 0)
                    if has(i, "finish"):
                        if s == 8:
                            wait(dve, sm["ssq_ready"], fin, 1, 1)
                            wait(dve, sm["msq_done"], fin, 1, 0)
                            nc.vector.tensor_copy(ssq[:, :], misc[:, 0:T]).then_inc(sm["ssq_copied"], 1)
                        if s == 12:
                            wait(dve, sm["t_copied"], fin, 1, 1)
                        if s in (12, 13):
                            wait(dve, sm["rsd"], fin, 1, 0)
                            statistics(fin, t_sb, stat["d"], mv["d"], "statd", "mvd", s - 12)
                    if has(i, "attend") and s in (26, 28):
                        quotient(i, 0, (s - 26) // 2)
                    if has(i, "post"):
                        if s in (4, 5):
                            quotient(post, 1, s - 4)
                        if s == 6:
                            wait(dve, sm["z_scaled"], post, 2, 2)
                            nc.vector.tensor_scalar(neg[:, :, :], z[:, :, :], 0.0, None, ALU.min
                                                    ).then_inc(sm["zneg_done"], 1)
                            wait(dve, sm["zneg_done"], post, 1, 1)
                            nc.vector.scalar_tensor_tensor(z[:, :, :], z[:, :, :], 0.0, neg[:, :, :],
                                                           ALU.max, ALU.add).then_inc(sm["z_done"], 1)
                        for first, second, n, src, ready in ((8, 9, "a", x1, "x1_done"), (14, 15, "b", a_out, "beta_done"),
                                                             (19, 20, "c", y[post.buf], "y_done")):
                            if s == first:
                                wait(dve, sm[ready], post, 1, 1)
                                statistics(post, src, stat[n], mv[n], "stat" + n, "mv" + n, 0)
                            if s == second:
                                statistics(post, src, stat[n], mv[n], "stat" + n, "mv" + n, 1)
                    if not has(i, "attend"):
                        last_turns(i, s)
                    if has(i, "ahead"):
                        if s == 0:
                            wait(dve, sm["v_ready"], ahead, 1, 1)
                            wait(dve, sm["bv_done"], Turn(0), 1, 1)
                            nc.vector.tensor_tensor(v_tok[:, :, :], misc_t, bv_v[:, :].unsqueeze(1).broadcast_to([P, T, D]),
                                                    ALU.add).then_inc(sm["v_added"], 1)
                        if s == 27:
                            wait(dve, sm["v_added"], ahead, 1, 1)
                            wait(dve, sm["valid_done"], ahead, 1, 1)
                            wait(dve, sm["summed"], ahead, STEPS, -STEPS)
                            if ahead.reg is None and ahead.offset == 0:
                                dve.wait_ge(sm["values_zeroed"], 1)
                            for i2 in range(2):
                                c = 16 * i2
                                last = nc.vector.tensor_tensor(
                                    v_only[ahead.buf][:, :, i2, :, c:c + HD],
                                    v_tok[:, :, 64 * i2:64 * i2 + 64].rearrange("p t (h c) -> p t h c", c=HD),
                                    valid[ahead.buf][:, :].unsqueeze(2).unsqueeze(3).broadcast_to([P, T, 8, HD]), ALU.mult)
                            last.then_inc(sm["v_done"], 1)
                    if has(i, "prepare"):
                        if s == 1:
                            wait(dve, sm["x_loaded"], prep, DMA, DMA)
                        if s in (1, 2):
                            wait(dve, sm["rs1_done"], prep, 1, 0)
                            statistics(prep, x_in, stat1, mv1, "stat1_done", "mv1_done", s - 1)
                        if s == 7:
                            wait(dve, sm["xn_done"], prep, 1, 1)
                            wait(dve, sm["xnT_ready"], prep, 1, 0)
                            nc.vector.tensor_scalar(xs[:, :, :], xn[:, :, :], -XN_BOUND, XN_BOUND, ALU.max, ALU.min
                                                    ).then_inc(sm["xs_done"], 1)
                            if prep.reg is None and prep.offset == 0:
                                setup_rows()
                        if s == 29:
                            wait(dve, sm["v_placed"], prep, 2, -2)
                            nc.vector.tensor_tensor(valid[prep.buf][:, :], rs1[:, 3, :], rs1[:, 3, :], ALU.is_equal
                                                    ).then_inc(sm["valid_done"], 1)
                        if s == 31 and prep.reg is None and prep.offset == 0:
                            setup_ff()

            turns(dve, body)

        @block.gpsimd
        def _(pool):
            nc.gpsimd.memset(ident[:, :], 0.0).then_inc(sm["ident_set"], 1)
            nc.gpsimd.memset(ident16[:, :], 0.0).then_inc(sm["ident_set"], 1)
            for n, e in enumerate((-0.5, 0.5, -1.0)):
                last = nc.gpsimd.memset(exponents[:, n, :], e)
            last.then_inc(sm["consts_set"], 1)
            nc.gpsimd.memset(ones[:, :], 1.0).then_inc(sm["ones_made"], 1)
            nc.gpsimd.memset(one_rows[:, :, :], 1.0).then_inc(sm["one_rows_set"], 1)
            pool.wait_ge(sm["ident_set"], 2)
            for m in (ident, ident16):
                nc.gpsimd.affine_select(out=m[:, :], in_=m[:, :], compare_op=ALU.not_equal, fill=1.0, base=0,
                                        pattern=[[-1, P]], channel_multiplier=1).then_inc(sm["ident_made"], 1)
            pool.wait_ge(sm["one_rows_set"], 1)
            for hp in range(2):
                last = nc.gpsimd.affine_select(out=one_rows[:, hp, :], in_=one_rows[:, hp, :], compare_op=ALU.is_ge,
                                               fill=0.0, base=(1, -2)[hp], pattern=[[0, S]],
                                               channel_multiplier=(-1, 1)[hp])
            last.then_inc(sm["one_rows_made"], 1)
            pool.wait_ge(sm["consts_set"], 1)

            def setup_values():
                for n in range(2):
                    nc.gpsimd.memset(v_one[n][:, :, :, :, :], 0.0)
                    nc.gpsimd.memset(v_only[n][:, :, :, :, :], 0.0)
                    last = nc.gpsimd.memset(one_only[n][:, :, :, :], 0.0)
                last.then_inc(sm["values_zeroed"], 1)

            def rsqrt_of(b, mv_, r, eps_sem, pow_sem, done):
                nc.gpsimd.tensor_scalar(r[:, 0, :], mv_[:, :, 1], LN_EPS, None, ALU.add)
                nc.gpsimd.tensor_scalar(r[:, 2, :], mv_[:, :, 0], -1.0, None, ALU.mult).then_inc(sm[eps_sem], 1)
                wait(pool, sm[eps_sem], b, 1, 1, setup)
                nc.gpsimd.tensor_tensor(r[:, 1, :], r[:, 0, :], exponents[:, 0, :], ALU.pow).then_inc(sm[pow_sem], 1)
                wait(pool, sm[pow_sem], b, 1, 1, setup)
                nc.gpsimd.tensor_tensor(r[:, 3, :], r[:, 2, :], r[:, 1, :], ALU.mult).then_inc(sm[done], 1)

            def mask(b, s):
                kt = (s // 2) % T
                wait(pool, sm["exp_done"], b, UNITS, s + 1, setup)
                wait(pool, sm["summed"], b, STEPS, s // 2 - RING // 2 + 1, setup)
                nc.gpsimd.affine_select(out=diag[s % RING][:, :, :], in_=probs[s % RING][:, :, kt * P:(kt + 1) * P],
                                        compare_op=ALU.is_ge, fill=0.0, base=0, pattern=[[0, 2], [-1, P]],
                                        channel_multiplier=1).then_inc(sm["masked"], 1)

            def split(b, n, s):
                if s == 0:
                    wait(pool, sm[("q_copied", "k_copied")[n]], b, 1, 1, setup)
                    nc.gpsimd.tensor_tensor(parts[:, 1, n, :], qk[:, n, :], parts[:, 0, n, :], ALU.subtract
                                            ).then_inc(sm["mid_done"], 1)
                if s == 1:
                    wait(pool, sm["mid_done"], b, 2, n + 1, setup)
                    nc.gpsimd.tensor_tensor(qk[:, n, :], qk[:, n, :], parts[:, 0, n, :], ALU.subtract
                                            ).then_inc(sm["mid_left"], 1)
                if s == 2:
                    wait(pool, sm["mid_left"], b, 2, n + 1, setup)
                    nc.gpsimd.tensor_tensor(parts[:, 2, n, :], qk[:, n, :], parts[:, 1, n, :], ALU.subtract
                                            ).then_inc(sm["low_done"], 1)

            def body(i):
                post, fin, prep, ahead = i.plus(-1), i.plus(-2), i.plus(2), i.plus(1)
                for s in range(UNITS):
                    if has(i, "prepare"):
                        if s == 5:
                            wait(pool, sm["mv1_done"], prep, 1, 1, setup)
                            wait(pool, sm["xn_done"], prep, 1, 0, setup)
                            wait(pool, sm["valid_done"], prep, 1, 0, setup)
                            rsqrt_of(prep, mv1, rs1, "eps1_done", "pow1_done", "rs1_done")
                        for n, slots in enumerate(((15, 17, 19), (25, 26, 27))):
                            if s in slots:
                                split(prep, n, slots.index(s))
                        if s == UNITS - 1 and prep.reg is None and prep.offset == 0:
                            setup_values()
                    if has(i, "finish"):
                        if 1 <= s < 1 + FT and (has(i, "attend") or s < 3):
                            f = s - 1
                            wait(pool, sm["gelu_done"], fin, 1, 1, setup)
                            wait(pool, sm["ssqf_ready"], fin, 1, 0, setup)
                            nc.gpsimd.tensor_tensor(h2[:, f, :], hT[:, f, :], hT[:, f, :], ALU.mult
                                                    ).then_inc(sm["h2_done"], 1)
                        if s == 9:
                            wait(pool, sm["ssq_copied"], fin, 1, 1, setup)
                            nc.gpsimd.tensor_scalar(rs_d[:, 0, :], ssq[:, :], 1.0 / (32 * FF), None, ALU.mult
                                                    ).then_inc(sm["msq_done"], 1)
                            wait(pool, sm["msq_done"], fin, 1, 1, setup)
                            nc.gpsimd.tensor_tensor(rs_d[:, 1, :], rs_d[:, 0, :], exponents[:, 1, :], ALU.pow
                                                    ).then_inc(sm["rmsh_done"], 1)
                        if s == 11:
                            wait(pool, sm["rmsh_done"], fin, 1, 1, setup)
                            nc.gpsimd.tensor_scalar(rs_d[:, 0, :], rs_d[:, 1, :], RMS_EPS, None, ALU.add
                                                    ).then_inc(sm["rmsh_eps"], 1)
                            wait(pool, sm["rmsh_eps"], fin, 1, 1, setup)
                            nc.gpsimd.tensor_tensor(rs_d[:, 2, :], rs_d[:, 0, :], exponents[:, 2, :], ALU.pow
                                                    ).then_inc(sm["invh_done"], 1)
                            wait(pool, sm["invh_done"], fin, 1, 1, setup)
                            nc.gpsimd.tensor_tensor(rs_d[:, 3, :], rs_d[:, 2, :], rs_d[:, 2, :], ALU.mult
                                                    ).then_inc(sm["sqh_done"], 1)
                        if s == 14:
                            wait(pool, sm["mvd"], fin, 1, 1, setup)
                            wait(pool, sm["sqh_done"], fin, 1, 1, setup)
                            nc.gpsimd.tensor_scalar(rs_d[:, 6, :], mv["d"][:, :, 0], -1.0, None, ALU.mult)
                            nc.gpsimd.tensor_tensor(rs_d[:, 0, :], rs_d[:, 3, :], mv["d"][:, :, 1], ALU.mult
                                                    ).then_inc(sm["vard_done"], 1)
                            wait(pool, sm["vard_done"], fin, 1, 1, setup)
                            nc.gpsimd.tensor_scalar(rs_d[:, 1, :], rs_d[:, 0, :], LN_EPS, None, ALU.add
                                                    ).then_inc(sm["epsd"], 1)
                            wait(pool, sm["epsd"], fin, 1, 1, setup)
                            nc.gpsimd.tensor_tensor(rs_d[:, 4, :], rs_d[:, 1, :], exponents[:, 0, :], ALU.pow
                                                    ).then_inc(sm["powd"], 1)
                        if s == 20:
                            wait(pool, sm["powd"], fin, 1, 1, setup)
                            nc.gpsimd.tensor_tensor(rs_d[:, 5, :], rs_d[:, 4, :], rs_d[:, 2, :], ALU.mult
                                                    ).then_inc(sm["scaled"], 1)
                            wait(pool, sm["scaled"], fin, 1, 1, setup)
                            nc.gpsimd.tensor_tensor(rs_d[:, 7, :], rs_d[:, 6, :], rs_d[:, 5, :], ALU.mult
                                                    ).then_inc(sm["rsd"], 1)
                        if s == 29 and has(i, "attend"):
                            wait(pool, sm["normd"], fin, 1, 1, setup)
                            wait(pool, sm["stored"], fin, DMA, 0, setup)
                            nc.gpsimd.tensor_tensor(o_sb[:, :, :], t_sb[:, :, :], y[fin.buf][:, :, :], ALU.add
                                                    ).then_inc(sm["o_done"], 1)
                    if has(i, "post"):
                        if s == 7 and has(i, "attend"):
                            wait(pool, sm["z_done"], post, 1, 1, setup)
                            wait(pool, sm["res_loaded"], post, 2 * DMA, 2 * DMA, setup)
                            wait(pool, sm["norma"], post, 1, 0, setup)
                            nc.gpsimd.tensor_tensor(x1[:, :, :], xn_res[:, :, :], z[:, :, :], ALU.add
                                                    ).then_inc(sm["x1_done"], 1)
                        if s == 10:
                            wait(pool, sm["mva"], post, 1, 1, setup)
                            rsqrt_of(post, mv["a"], rs["a"], "epsa", "powa", "rsa")
                        if s == 12 and has(i, "attend"):
                            wait(pool, sm["norma"], post, 1, 1, setup)
                            nc.gpsimd.tensor_tensor(a_out[:, :, :], a_out[:, :, :],
                                                    gamma_b[:, :].unsqueeze(1).broadcast_to([P, T, D]), ALU.mult
                                                    ).then_inc(sm["gam_done"], 1)
                        if s == 13 and has(i, "attend"):
                            wait(pool, sm["gam_done"], post, 1, 1, setup)
                            nc.gpsimd.tensor_tensor(a_out[:, :, :], a_out[:, :, :],
                                                    beta_b[:, :].unsqueeze(1).broadcast_to([P, T, D]), ALU.add
                                                    ).then_inc(sm["beta_done"], 1)
                        if s == 16:
                            wait(pool, sm["mvb"], post, 1, 1, setup)
                            rsqrt_of(post, mv["b"], rs["b"], "epsb", "powb", "rsb")
                        if s == 18 and has(i, "attend"):
                            wait(pool, sm["normb"], post, 1, 1, setup)
                            wait(pool, sm["o_done"], post, 1, -1, setup)
                            nc.gpsimd.tensor_tensor(y[post.buf][:, :, :], x_res[:, :, :], a_out[:, :, :], ALU.add
                                                    ).then_inc(sm["y_done"], 1)
                        r = rs["c"]
                        if s == 21:
                            wait(pool, sm["mvc"], post, 1, 1, setup)
                            nc.gpsimd.tensor_scalar(r[:, 0, :], mv["c"][:, :, 1], LN_EPS, None, ALU.add)
                            nc.gpsimd.tensor_scalar(r[:, 4, :], mv["c"][:, :, 0], -1.0, None, ALU.mult)
                            nc.gpsimd.tensor_scalar(r[:, 1, :], mv["c"][:, :, 1], 1.0, None, ALU.mult
                                                    ).then_inc(sm["epsc"], 1)
                            wait(pool, sm["epsc"], post, 1, 1, setup)
                            nc.gpsimd.tensor_tensor(r[:, 2:4, :], r[:, 0:2, :], exponents[:, 0:2, :], ALU.pow
                                                    ).then_inc(sm["powc"], 1)
                        if s == 22:
                            wait(pool, sm["powc"], post, 1, 1, setup)
                            nc.gpsimd.tensor_tensor(r[:, 0, :], r[:, 2, :], r[:, 3, :], ALU.mult
                                                    ).then_inc(sm["mulc"], 1)
                            wait(pool, sm["mulc"], post, 1, 1, setup)
                            nc.gpsimd.tensor_scalar(r[:, 1, :], r[:, 0, :], RMS_EPS, None, ALU.add
                                                    ).then_inc(sm["addc"], 1)
                        if s == 23:
                            wait(pool, sm["addc"], post, 1, 1, setup)
                            nc.gpsimd.tensor_tensor(r[:, 0, :], r[:, 1, :], exponents[:, 2, :], ALU.pow
                                                    ).then_inc(sm["invc"], 1)
                            wait(pool, sm["invc"], post, 1, 1, setup)
                            nc.gpsimd.tensor_tensor(r[:, 3, :], r[:, 0, :], r[:, 2, :], ALU.mult
                                                    ).then_inc(sm["scalec"], 1)
                            wait(pool, sm["scalec"], post, 1, 1, setup)
                            nc.gpsimd.tensor_tensor(r[:, 5, :], r[:, 4, :], r[:, 3, :], ALU.mult
                                                    ).then_inc(sm["rsc"], 1)

                    if s and has(i, "attend"):
                        mask(i, s - 1)
                    if s == 0 and has(i, "post"):
                        mask(post, UNITS - 1)

            turns(pool, body)


_INS = ["L0_attn_embedded", "L0_attn_Wq", "L0_attn_bq", "L0_attn_Wk", "L0_attn_bk", "L0_attn_Wv", "L0_attn_bv",
        "L0_attn_gamma", "L0_attn_beta", "L0_ffn_w_up", "L0_ffn_w_down"]


def kernel(**inputs):
    import concourse.bacc as bacc
    from concourse.bass_utils import run_bass_kernel_spmd

    nc = bacc.Bacc("TRN2", target_bir_lowering=False, num_devices=1)
    arrays, args = {}, []
    for name in _INS:
        a = np.ascontiguousarray(inputs[name])
        arrays[f"in_{name}_dram"] = a
        args.append(nc.dram_tensor(f"in_{name}_dram", a.shape, mybir.dt.from_np(a.dtype), kind="ExternalInput").ap())
    args.append(nc.dram_tensor("out_0_dram", (B, S, D), F32, kind="ExternalOutput").ap())
    build(nc, *args)
    r = run_bass_kernel_spmd(nc, [arrays], core_ids=[0])
    return r.results[0]["out_0_dram"]
```
